# Optimizing a Trainium2 kernel written in Bass

```python
import numpy as np
import jax
import jax.numpy as jnp

def _softmax(x, axis=-1):
    return jax.nn.softmax(x, axis=axis)

def _gelu(x):
    return jax.nn.gelu(x, approximate=True)

def _silu(x):
    return jax.nn.silu(x)

def _sigmoid(x):
    return jax.nn.sigmoid(x)

def _layernorm(x, axis=-1, eps=1e-05):
    m = jnp.mean(x, axis=axis, keepdims=True)
    v = jnp.var(x, axis=axis, keepdims=True)
    return (x - m) / jnp.sqrt(v + eps)

def _scatter_add(tgt, idx, src, axis=0):
    return tgt.at[idx].add(src)

def _segment_sum(src, seg, n):
    return jax.ops.segment_sum(src, seg, n)
kernel_name = 'mk_perceiver_d1_seqx_r2_e7ced1'

def setup_inputs(seed: int=0):
    np.random.seed(seed)
    _w = jnp.asarray

    def _rec_inputs():
        import jax
        import jax.numpy as jnp
        _rk = jax.random.key(seed)
        x = 7.22e-05 + 1 * jax.random.normal(jax.random.fold_in(_rk, 1), (16, 64, 512), jnp.float32)
        _lenS = 64 - jax.random.randint(jax.random.fold_in(_rk, 7), (16,), 0, max(1, 64 // 4) + 1, jnp.int32)
        _lenS2 = 512 - jax.random.randint(jax.random.fold_in(_rk, 8), (16,), 0, max(1, 512 // 4) + 1, jnp.int32)
        _ctx_768P = jax.random.normal(jax.random.fold_in(_rk, 11), (16, 16, 384), jnp.float32)
        _ctx_768c = jax.random.dirichlet(jax.random.fold_in(_rk, 511), 0.3 * jnp.ones((16,), jnp.float32), (16, 512))
        _ctx_768t = jnp.einsum('bsk,bkd->bsd', _ctx_768c, _ctx_768P)
        _ctx_768t = _ctx_768t * jax.lax.rsqrt(jnp.mean(jnp.square(_ctx_768t)) + 1e-12) * 0.953939
        ctx_768 = -0.000191848 + 0.999787 * (_ctx_768t + 0.3 * jax.random.normal(jax.random.fold_in(_rk, 611), (16, 512, 384), jnp.float32))
        return (x, ctx_768)
    x, ctx_768 = _rec_inputs()

    def _L0_xattn_setup():
        import math
        import jax, jax.numpy as jnp
        import numpy as np
        B, SQ, SKV = (4, 1024, 1024)
        D_EMBED, D_CROSS, D_ATT, N_HEADS = (512, 384, 512, 16)
        D_HEAD = D_ATT // N_HEADS

        def _split_heads(t):
            b, s, _ = t.shape
            return t.reshape(b, s, N_HEADS, D_HEAD).transpose(0, 2, 1, 3)
        key = jax.random.key(seed)
        ks = jax.random.split(key, 10)
        s_e = 1.0 / math.sqrt(D_EMBED)
        s_c = 1.0 / math.sqrt(D_CROSS)
        s_a = 1.0 / math.sqrt(D_ATT)
        return {'x': jax.random.normal(ks[0], (B, SQ, D_EMBED), jnp.float32), 'y': jax.random.normal(ks[1], (B, SKV, D_CROSS), jnp.float32), 'Wq': jax.random.normal(ks[2], (D_EMBED, D_ATT), jnp.float32) * s_e, 'bq': jax.random.normal(ks[3], (D_ATT,), jnp.float32) * 0.01, 'Wk': jax.random.normal(ks[4], (D_CROSS, D_ATT), jnp.float32) * s_c, 'bk': jax.random.normal(ks[5], (D_ATT,), jnp.float32) * 0.01, 'Wv': jax.random.normal(ks[6], (D_CROSS, D_ATT), jnp.float32) * s_c, 'bv': jax.random.normal(ks[7], (D_ATT,), jnp.float32) * 0.01, 'Wo': jax.random.normal(ks[8], (D_ATT, D_EMBED), jnp.float32) * s_a, 'bo': jax.random.normal(ks[9], (D_EMBED,), jnp.float32) * 0.01}
    _L0_xattn_all = _L0_xattn_setup()
    _L0_xattn_in = {k: v for k, v in _L0_xattn_all.items() if k in ('Wq', 'bq', 'Wk', 'bk', 'Wv', 'bv', 'Wo', 'bo')}
    del _L0_xattn_all

    def _L0_attn_setup():
        import jax, jax.numpy as jnp
        import numpy as np
        PI = float(np.pi)
        LN_EPS = 1e-05
        COS_EPS = 1e-06
        D_HIDDEN, N_HEADS, D_HEAD, D_MLP = (512, 16, 64, 2048)
        B, T = (4, 1024)

        def _xavier(key, shape):
            rf = 1
            for s in shape[2:]:
                rf *= s
            fan_in, fan_out = (shape[1] * rf, shape[0] * rf)
            bound = float(np.sqrt(6.0 / (fan_in + fan_out)))
            return jax.random.uniform(key, shape, jnp.float32, -bound, bound)

        def _layer_norm(x, w, b):
            mu = jnp.mean(x, axis=-1, keepdims=True)
            var = jnp.mean(jnp.square(x - mu), axis=-1, keepdims=True)
            return (x - mu) * jax.lax.rsqrt(var + LN_EPS) * w + b

        def _cos_attention(y, W_Q, W_K, W_V, W_O):
            q = jnp.einsum('btd,idh->btih', y, W_Q)
            k = jnp.einsum('btd,idh->btih', y, W_K)
            V = jnp.einsum('btd,idh->btih', y, W_V)
            q = jnp.tanh(q) * (PI / 4)
            k = jnp.tanh(k) * (PI / 4)
            cos_k, sin_k = (jnp.cos(k), jnp.sin(k))
            cos_KV = jnp.cumsum(cos_k * V, axis=1)
            sin_KV = jnp.cumsum(sin_k * V, axis=1)
            cos_Q, sin_Q = (jnp.cos(q), jnp.sin(q))
            heads = cos_Q * cos_KV + sin_Q * sin_KV
            cos_K = jnp.cumsum(cos_k, axis=1)
            sin_K = jnp.cumsum(sin_k, axis=1)
            denom = cos_Q * cos_K + sin_Q * sin_K + COS_EPS
            heads = heads / denom
            return jnp.einsum('dhi,btih->btd', W_O, heads)
        key = jax.random.key(seed)
        ks = jax.random.split(key, 10)
        x = jax.random.normal(ks[0], (B, T, D_HIDDEN), jnp.float32)
        W_Q = _xavier(ks[1], (N_HEADS, D_HIDDEN, 1))
        W_K = _xavier(ks[2], (N_HEADS, D_HIDDEN, 1))
        W_V = _xavier(ks[3], (N_HEADS, D_HIDDEN, D_HEAD))
        W_O = _xavier(ks[4], (D_HIDDEN, D_HEAD, N_HEADS))
        ln1_w = jnp.ones((D_HIDDEN,), jnp.float32)
        ln1_b = jnp.zeros((D_HIDDEN,), jnp.float32)
        ln2_w = jnp.ones((D_HIDDEN,), jnp.float32)
        ln2_b = jnp.zeros((D_HIDDEN,), jnp.float32)
        s1 = 1.0 / np.sqrt(D_HIDDEN)
        s2 = 1.0 / np.sqrt(D_MLP)
        W1 = jax.random.uniform(ks[5], (D_HIDDEN, D_MLP), jnp.float32, -s1, s1)
        b1 = jax.random.uniform(ks[6], (D_MLP,), jnp.float32, -s1, s1)
        W2 = jax.random.uniform(ks[7], (D_MLP, D_HIDDEN), jnp.float32, -s2, s2)
        b2 = jax.random.uniform(ks[8], (D_HIDDEN,), jnp.float32, -s2, s2)
        return {'x': x, 'W_Q': W_Q, 'W_K': W_K, 'W_V': W_V, 'W_O': W_O, 'ln1_w': ln1_w, 'ln1_b': ln1_b, 'ln2_w': ln2_w, 'ln2_b': ln2_b, 'W1': W1, 'b1': b1, 'W2': W2, 'b2': b2}
    _L0_attn_all = _L0_attn_setup()
    _L0_attn_in = {k: v for k, v in _L0_attn_all.items() if k in ('W_Q', 'W_K', 'W_V', 'W_O', 'ln1_w', 'ln1_b', 'ln2_w', 'ln2_b', 'W1', 'b1', 'W2', 'b2')}
    del _L0_attn_all

    def _L0_ffn_setup():
        import jax, jax.numpy as jnp
        import numpy as np
        B, K, D = (128, 32, 512)
        E = 32
        H = int(D * 0.25)

        def _rsqrt_uniform(key, shape, d):
            bound = d ** (-0.5)
            return jax.random.uniform(key, shape, jnp.float32, -bound, bound)
        key = jax.random.key(seed)
        ks = jax.random.split(key, 7)
        return {'x': jax.random.normal(ks[0], (B, K, D), jnp.float32), 'router_w': _rsqrt_uniform(ks[1], (E, D), D), 'router_b': _rsqrt_uniform(ks[2], (E,), D), 'weights1': _rsqrt_uniform(ks[3], (E, D, H), H), 'bias1': _rsqrt_uniform(ks[4], (E, H), H), 'weights2': _rsqrt_uniform(ks[5], (E, H, D), D), 'bias2': _rsqrt_uniform(ks[6], (E, D), D)}
    _L0_ffn_all = _L0_ffn_setup()
    _L0_ffn_in = {k: v for k, v in _L0_ffn_all.items() if k in ('router_w', 'router_b', 'weights1', 'bias1', 'weights2', 'bias2')}
    del _L0_ffn_all
    return {'x': x, 'ctx_768': ctx_768, 'L0_xattn_Wq': _L0_xattn_in['Wq'], 'L0_xattn_bq': _L0_xattn_in['bq'], 'L0_xattn_Wk': _L0_xattn_in['Wk'], 'L0_xattn_bk': _L0_xattn_in['bk'], 'L0_xattn_Wv': _L0_xattn_in['Wv'], 'L0_xattn_bv': _L0_xattn_in['bv'], 'L0_xattn_Wo': _L0_xattn_in['Wo'], 'L0_xattn_bo': _L0_xattn_in['bo'], 'L0_attn_W_Q': _L0_attn_in['W_Q'], 'L0_attn_W_K': _L0_attn_in['W_K'], 'L0_attn_W_V': _L0_attn_in['W_V'], 'L0_attn_W_O': _L0_attn_in['W_O'], 'L0_attn_ln1_w': _L0_attn_in['ln1_w'], 'L0_attn_ln1_b': _L0_attn_in['ln1_b'], 'L0_attn_ln2_w': _L0_attn_in['ln2_w'], 'L0_attn_ln2_b': _L0_attn_in['ln2_b'], 'L0_attn_W1': _L0_attn_in['W1'], 'L0_attn_b1': _L0_attn_in['b1'], 'L0_attn_W2': _L0_attn_in['W2'], 'L0_attn_b2': _L0_attn_in['b2'], 'L0_ffn_router_w': _L0_ffn_in['router_w'], 'L0_ffn_router_b': _L0_ffn_in['router_b'], 'L0_ffn_weights1': _L0_ffn_in['weights1'], 'L0_ffn_bias1': _L0_ffn_in['bias1'], 'L0_ffn_weights2': _L0_ffn_in['weights2'], 'L0_ffn_bias2': _L0_ffn_in['bias2']}

def reference(x, ctx_768, L0_xattn_Wq, L0_xattn_bq, L0_xattn_Wk, L0_xattn_bk, L0_xattn_Wv, L0_xattn_bv, L0_xattn_Wo, L0_xattn_bo, L0_attn_W_Q, L0_attn_W_K, L0_attn_W_V, L0_attn_W_O, L0_attn_ln1_w, L0_attn_ln1_b, L0_attn_ln2_w, L0_attn_ln2_b, L0_attn_W1, L0_attn_b1, L0_attn_W2, L0_attn_b2, L0_ffn_router_w, L0_ffn_router_b, L0_ffn_weights1, L0_ffn_bias1, L0_ffn_weights2, L0_ffn_bias2):
    import jax
    import jax.numpy as jnp

    def _L0_xattn_ref(x, y, Wq, bq, Wk, bk, Wv, bv, Wo, bo):
        import math
        import jax, jax.numpy as jnp
        import numpy as np
        B, SQ, SKV = (4, 1024, 1024)
        D_EMBED, D_CROSS, D_ATT, N_HEADS = (512, 384, 512, 16)
        D_HEAD = D_ATT // N_HEADS

        def _split_heads(t):
            b, s, _ = t.shape
            return t.reshape(b, s, N_HEADS, D_HEAD).transpose(0, 2, 1, 3)
        q = _split_heads(x @ Wq + bq)
        k = _split_heads(y @ Wk + bk)
        v = _split_heads(y @ Wv + bv)
        scale = 1.0 / math.sqrt(D_HEAD)
        scores = jnp.einsum('bhqd,bhkd->bhqk', q, k) * scale
        weights = jax.nn.softmax(scores, axis=-1)
        out = jnp.einsum('bhqk,bhkd->bhqd', weights, v)
        out = out.transpose(0, 2, 1, 3).reshape(x.shape[0], x.shape[1], D_ATT)
        return out @ Wo + bo

    def _L0_attn_ref(x, W_Q, W_K, W_V, W_O, ln1_w, ln1_b, ln2_w, ln2_b, W1, b1, W2, b2):
        import jax, jax.numpy as jnp
        import numpy as np
        PI = float(np.pi)
        LN_EPS = 1e-05
        COS_EPS = 1e-06
        D_HIDDEN, N_HEADS, D_HEAD, D_MLP = (512, 16, 64, 2048)
        B, T = (4, 1024)

        def _xavier(key, shape):
            rf = 1
            for s in shape[2:]:
                rf *= s
            fan_in, fan_out = (shape[1] * rf, shape[0] * rf)
            bound = float(np.sqrt(6.0 / (fan_in + fan_out)))
            return jax.random.uniform(key, shape, jnp.float32, -bound, bound)

        def _layer_norm(x, w, b):
            mu = jnp.mean(x, axis=-1, keepdims=True)
            var = jnp.mean(jnp.square(x - mu), axis=-1, keepdims=True)
            return (x - mu) * jax.lax.rsqrt(var + LN_EPS) * w + b

        def _cos_attention(y, W_Q, W_K, W_V, W_O):
            q = jnp.einsum('btd,idh->btih', y, W_Q)
            k = jnp.einsum('btd,idh->btih', y, W_K)
            V = jnp.einsum('btd,idh->btih', y, W_V)
            q = jnp.tanh(q) * (PI / 4)
            k = jnp.tanh(k) * (PI / 4)
            cos_k, sin_k = (jnp.cos(k), jnp.sin(k))
            cos_KV = jnp.cumsum(cos_k * V, axis=1)
            sin_KV = jnp.cumsum(sin_k * V, axis=1)
            cos_Q, sin_Q = (jnp.cos(q), jnp.sin(q))
            heads = cos_Q * cos_KV + sin_Q * sin_KV
            cos_K = jnp.cumsum(cos_k, axis=1)
            sin_K = jnp.cumsum(sin_k, axis=1)
            denom = cos_Q * cos_K + sin_Q * sin_K + COS_EPS
            heads = heads / denom
            return jnp.einsum('dhi,btih->btd', W_O, heads)
        y = _layer_norm(x, ln1_w, ln1_b)
        x = x + _cos_attention(y, W_Q, W_K, W_V, W_O)
        y = _layer_norm(x, ln2_w, ln2_b)
        mlp = jnp.dot(jax.nn.gelu(jnp.dot(y, W1) + b1), W2) + b2
        return x + mlp

    def _L0_ffn_ref(x, router_w, router_b, weights1, bias1, weights2, bias2):
        import jax, jax.numpy as jnp
        import numpy as np
        B, K, D = (128, 32, 512)
        E = 32
        H = int(D * 0.25)

        def _rsqrt_uniform(key, shape, d):
            bound = d ** (-0.5)
            return jax.random.uniform(key, shape, jnp.float32, -bound, bound)
        b, k, d = x.shape
        x_flat = x.reshape(-1, d)
        n = x_flat.shape[0]
        logits = x_flat @ router_w.T + router_b
        routed_idx = jnp.argmax(logits, axis=-1)

        def expert_mlp(w1, b1, w2, b2):
            h = jax.nn.relu(x_flat @ w1 + b1)
            return jax.nn.relu(h @ w2 + b2)
        y_all = jax.vmap(expert_mlp)(weights1, bias1, weights2, bias2)
        out_flat = y_all[routed_idx, jnp.arange(n)]
        return out_flat.reshape(b, k, d)
    x = x + _L0_xattn_ref(_layernorm(x, axis=-1), ctx_768, L0_xattn_Wq, L0_xattn_bq, L0_xattn_Wk, L0_xattn_bk, L0_xattn_Wv, L0_xattn_bv, L0_xattn_Wo, L0_xattn_bo)
    x = x + _L0_attn_ref(_layernorm(x, axis=-1), L0_attn_W_Q, L0_attn_W_K, L0_attn_W_V, L0_attn_W_O, L0_attn_ln1_w, L0_attn_ln1_b, L0_attn_ln2_w, L0_attn_ln2_b, L0_attn_W1, L0_attn_b1, L0_attn_W2, L0_attn_b2)
    x = x + _L0_ffn_ref(_layernorm(x, axis=-1), L0_ffn_router_w, L0_ffn_router_b, L0_ffn_weights1, L0_ffn_bias1, L0_ffn_weights2, L0_ffn_bias2)
    return x

_drawn_inputs = setup_inputs


def setup_inputs(seed=0):
    import zlib

    import numpy as np

    out = dict(_drawn_inputs(seed))
    spreads = {'L0_attn_ln1_w': (1.0, 0.6),
     'L0_attn_ln1_b': (0.0, 0.8),
     'L0_attn_ln2_w': (1.0, 0.6),
     'L0_attn_ln2_b': (0.0, 0.653)}
    factors = {'L0_xattn_bq': 26.34,
     'L0_xattn_bk': 64.0,
     'L0_xattn_bv': 5.5,
     'L0_xattn_bo': 4.841,
     'L0_attn_W_Q': 27.667,
     'L0_attn_W_K': 21.842,
     'L0_attn_b1': 8.0,
     'L0_attn_b2': 7.019,
     'L0_ffn_router_b': 3.214,
     'L0_ffn_bias1': 8.0,
     'L0_ffn_bias2': 6.911}
    for name, (base, spread) in spreads.items():
        noise = np.random.default_rng([zlib.crc32(name.encode()), seed]).standard_normal(out[name].shape)
        drawn = base * np.exp(spread * noise) if base else spread * noise
        out[name] = jnp.asarray(drawn.astype(out[name].dtype))
    for name, factor in factors.items():
        out[name] = (out[name] * factor).astype(out[name].dtype)
    return out
```

```python
import concourse.bass as bass
from concourse import mybir
from concourse.alu_op_type import AluOpType as ALU
import numpy as np

F32, F32R = mybir.dt.float32, mybir.dt.float32r
ACT = mybir.ActivationFunctionType
AX = mybir.AxisListType.X


def build(nc, x, ctxT, Wq, bq, Wk, bk, Wv, bv, Wo, bo, WQ, WK, WV, WO, ln1w, ln1b, ln2w, ln2b, W1, b1, W2, b2,
          rw, rb, E1, e1, E2, e2, consts, out, dbg=None):
    P = 128
    NB, SQ, D = 16, 64, 512
    SK, DC = ctxT.shape[2], ctxT.shape[1]
    T = NB * SQ // P
    KD, KC = D // P, DC // P
    NH, DH = 16, 32
    HG = D // P
    EPS = 1e-5
    SCALE = float(DH) ** -0.5

    from contextlib import ExitStack
    with ExitStack() as ctx:
        def sb(name, cols, dt=F32):
            return ctx.enter_context(nc.sbuf_tensor(name, [P, cols], dt))

        def ps(name):
            return ctx.enter_context(nc.psum_tensor(name, [P, 512], F32))

        def sem(name):
            return ctx.enter_context(nc.semaphore(name))

        R = sb("split_arena", 140 * 256, F32R)
        F = sb("plain_arena", 64 * 256, F32)

        def at(arena, kb, *shape):
            n = int(np.prod(shape))
            v = arena[:, kb * 256:kb * 256 + n]
            if len(shape) == 1:
                return v
            names = "abcde"[:len(shape)]
            return v.rearrange(f"p ({' '.join(names)}) -> p {' '.join(names)}",
                               **{c: s for c, s in zip(names[1:], shape[1:])})

        wk = at(R, 0, 2, KC, D)
        wv = at(R, 12, 2, KC, D)
        y = at(R, 24, 2, 2, KC, SK)
        kT = at(R, 48, 2, HG, SK)
        v = at(R, 64, 2, SK // P, D)
        pT = [at(R, kb, 2, 512) for kb in (80, 84, 128, 132)]
        qbd = at(R, 88, 2, 2, HG, P)
        xnT = at(R, 48, 2, KD, T * P)
        wq = at(R, 80, 2, KD, D)

        aT = at(R, 96, 2, HG, T * P)

        xs = at(F, 0, T, D)
        qT = at(F, 16, HG, T * P)
        probs = at(F, 32, 8, SK)
        wq_raw = at(F, 32, KD, D)
        xn = at(F, 40, 2, D)
        yraw = at(F, 48, 2, KC, SK)
        wk_raw = at(F, 16, KC, D)
        wv_raw = at(F, 22, KC, D)
        bo_bc = at(F, 62, D)
        attnT = at(F, 60, 2, HG, SQ)

        wo = at(R, 0, 2, KD, D)
        yT = [at(R, 0, 2, KD, 512), at(R, 96, 2, KD, 512)]
        wV = at(R, 16, 2, KD, 1024)
        wO = at(R, 48, 2, 8, D)
        wQK = at(R, 80, 2, 2, KD, P)
        bd = at(R, 88, 2, 512)
        v2 = at(R, 112, 2, 1024)
        A = at(R, 120, 2, 2, 512)
        hT = at(R, 128, 2, 8, P)
        C = [at(R, 136, 2, 512), at(R, 92, 2, 512)]
        zn = at(F, 16, T, D)
        wraw = at(F, 32, 2, 1024)
        th = at(F, 40, 2, 512)
        yF = at(F, 44, 2, 512)
        den = yF
        z = at(F, 48, T, D)
        At = at(F, 16, 2, 512)
        b2_bc = at(F, 42, D)

        w1c = at(R, 16, 2, 2, 512)
        w2c = at(R, 24, 2, 2, 512)
        hh = at(R, 32, 2, 2, 512)
        rws = at(R, 40, 2, KD, 32)
        e2s = at(R, 41, 2, D)
        oneh = at(R, 45, 1024)
        didx = at(R, 49, P)
        w1raw = at(F, 32, 2, 512)
        w2raw = at(F, 36, 2, 512)
        hF = at(F, 40, 2, 512)
        idx = at(F, 44, 1024)
        rw_raw = at(F, 50, KD, 32)
        e2_raw = at(F, 48, D)

        bq_s, bk_s, bv_s = sb("bq_s", HG), sb("bk_s", HG), sb("bv_s", HG)
        cs = sb("constants", consts.shape[1])
        ident, causal = cs[:, 0:P], cs[:, P:2 * P]
        o = 2 * P
        enum, half, mask4, line = cs[:, o:o + 32], cs[:, o + 32:o + 34], cs[:, o + 34:o + 38], cs[:, o + 40:o + 44]
        quarter = cs[:, o + 38:o + 39]
        onesr = ctx.enter_context(nc.sbuf_tensor("ones_r", [P, P], F32R))
        cols = sb("columns", 4 * KD + 16 + 32)
        l1w, l1b, l2w, l2b = (cols[:, 4 * i:4 * i + 4] for i in range(4))
        b1s, e1s = cols[:, 16:32], cols[:, 32:64]
        rbs = sb("rbs", 32)
        eps_c = sb("eps_c", 1)
        top, topi = sb("top8", 16), ctx.enter_context(nc.sbuf_tensor("top8i", [P, 16], mybir.dt.uint32))
        lg = sb("logits", 64)
        idf = sb("idf", 2)
        st, mv = sb("st", 6 * 2), sb("mv", 2 * T)
        mvv = mv[:].rearrange("p (t c) -> p t c", c=2)
        pw, rstd = sb("pw", T), sb("rstd", T)
        mx, nmx, sums, rs = sb("mx", 8), sb("nmx", 8), sb("sums", 8), sb("rs", 8)

        pb = [ps(f"bank{i}") for i in range(8)]
        KV, SC, TR = pb[0:2], pb[2:4], pb[5:7]
        RING = [pb[i] for i in (2, 3, 5, 6)]
        PV = [pb[4], pb[7]]

        names = """x_in0 x_in1 x_in2 x_in3 wq_in wk_in wv_in bias_in  ms_ok st_ok mv_ok abs_ok cos_ok eps_set h_f eps_ok rstd_ok xn_ok xnT_mm
          xnT_hi xnT_lo q_mm q_ok wq_hi wq_lo wkv_hi wkv_lo y_in0 y_in1 y_hi y_lo kv_mm kv_hi kv_lo
          qbd_hi qbd_ok s_mm mx_ok nmx_ok exp_ok rs_ok norm_ok cs_in bo_in cols_in aT_hi aT_lo xb_ok w_in0 w_in1 wb_hi wb_lo o_mm x1_ok ln_st ln_mv ln_eps ln_pow ln_out b2_in b2_ok t_mm y_f y_hi2 y_lo2 qk_mm th_ok line_ok c_hi c_lo v2_mm v2_hi v2_lo bd_ok a_mm a_ok a_hi a_lo nd_mm den_ok rec_ok hd_ok h_hi h_lo wo2_mm z2_ok base_ok w1_in0 w1_in1 w2_in0 w2_in1 w1_hi w1_lo w2_hi w2_lo hmm hact hmask hh_hi hh_lo f_mm x3_ok rw_in r_hi r_lo lg_mm lg_ok top_ok topi_ok id_ok di_ok idx_mm idx_ok one_ok onesr_ok fin_ok fin_out0 fin_out1 fin_in tr_mm pT_hi pT_lo pv_mm pv_out pv_out2 out_sem""".split()
        S = {n: sem(n) for n in names}
        block = ctx.enter_context(nc.Block())
        LOOPS = (NB - 2) // 2

        def over_batches(eng, body):
            body(0, 0)
            body(1, 1)
            with eng.Fori(0, LOOPS) as i:
                body(2 * i + 2, 0)
                body(2 * i + 3, 1)


        pieces = []
        for k in range(KD):
            pieces.append((Wo[k * P:(k + 1) * P, :], [wo[:, s_, k] for s_ in range(2)], D))
        for kind, W_ in enumerate((WK, WQ)):
            for k in range(KD):
                pieces.append((W_[k * P:(k + 1) * P, :], [wQK[:, kind, s_, k] for s_ in range(2)], P))
        for k in range(KD):
            pieces.append((WV[k * P:(k + 1) * P, :], [wV[:, s_, k] for s_ in range(2)], 1024))
        for k in range(8):
            pieces.append((WO[k * P:(k + 1) * P, :], [wO[:, s_, k] for s_ in range(2)], D))
        N_WO, N_QK, N_V, N_O = 4, 12, 16, 24
        OB = [0, 1, 2, 3, 4, 0, 1, 2]
        NT = [0, 1, 2, 3]
        parts = [(W1.rearrange("(k p) (c n) -> c p k n", p=P, n=P), W2.rearrange("(c p) n -> c p n", p=P), b1s, 16, 0),
                 (E1.rearrange("e (k p) n -> e p k n", p=P), E2, e1s, 32, 32)]

        def chunk_loop(eng, n, body):
            body(0, 0)
            with eng.Fori(0, (n - 2) // 2) as i:
                body(2 * i + 1, 1)
                body(2 * i + 2, 0)
            body(n - 1, 1)

        def source(w, c):
            return w[c] if isinstance(c, int) else w[bass.ds(c, 1)].rearrange(
                "c p k n -> (c p) k n" if len(w.shape) == 4 else "c p n -> (c p) n")

        def weight_loop(eng, part, h, hidden, split1, split2):
            n = parts[part][3]
            if part == 0 and h == 0:
                split1(part, 0, 0, 0)
                split1(part, 0, 1, 1)
                split2(part, 0, 0, 0)

            def step(c, par):
                hidden(part, h, c, par)
                split1(part, h, c + 2, par)
                split2(part, h, c + 1, 1 - par)
            step(0, 0)
            step(1, 1)
            with eng.Fori(1, (n - 2) // 2) as i:
                step(2 * i, 0)
                step(2 * i + 1, 1)
            nxt = {(0, 0): (0, 1), (0, 1): (1, 0), (1, 0): (1, 1), (1, 1): None}[part, h]
            hidden(part, h, n - 2, 0)
            if nxt:
                split1(*nxt, 0, 0)
            split2(part, h, n - 1, 1)
            hidden(part, h, n - 1, 1)
            if nxt:
                split1(*nxt, 1, 1)
                split2(*nxt, 0, 0)

        def total(part, h):
            return parts[part][4] + parts[part][3] * h

        def sp_tail(sp):
            for n, (src, _, w) in enumerate(pieces):
                if n < 2:
                    sp.wait_ge(S["tr_mm"], 8 * NB)
                else:
                    sp.wait_ge(S["wb_lo"], n - 1)
                sp.dma_start(wraw[:, n % 2, 0:w], src).then_inc(S[f"w_in{n % 2}"], 16)
            sp.wait_ge(S["a_lo"], 4 * T)
            sp.wait_ge(S["c_lo"], 4)
            sp.dma_start(b2_bc, b2.partition_broadcast(P)).then_inc(S["b2_in"], 16)
            def load1(part, h, c, par):
                j = total(part, h)
                if isinstance(c, int) and j + c < 2:
                    sp.wait_ge(S["wb_lo"], N_O)
                else:
                    sp.wait_ge(S["w1_lo"], c + (j - 1))
                sp.dma_start(w1raw[:, par].rearrange("p (k n) -> p k n", k=KD), source(parts[part][0], c)).then_inc(S[f"w1_in{par}"], 16)

            def load2(part, h, c, par):
                j = total(part, h)
                if not (isinstance(c, int) and j + c < 2):
                    sp.wait_ge(S["w2_lo"], c + (j - 1))
                sp.dma_start(w2raw[:, par], source(parts[part][1], c)).then_inc(S[f"w2_in{par}"], 16)
            for part in range(2):
                for h in range(2):
                    weight_loop(sp, part, h, lambda *_: None, load1, load2)
                    if part == 0 and h == 1:
                        sp.wait_ge(S["x3_ok"], T)
                        sp.dma_start(rw_raw, rw.rearrange("(k p) n -> p k n", p=P)).then_inc(S["rw_in"], 16)
                        sp.dma_start(e2_raw[0:32], e2).then_inc(S["rw_in"], 16)
            for t in range(T):
                sp.wait_ge(S["fin_out1"], t + 1)
                sp.dma_start(out.rearrange("(t p) d -> p t d", p=P)[:, t], xs[:, t]).then_inc(S["out_sem"], 16)
            sp.wait_ge(S["out_sem"], 16 * T)

        def pool_tail(pool):
            g = nc.gpsimd
            def pieces_to(a_, b_):
                for n in range(a_, b_):
                    _, (hi, lo), w = pieces[n]
                    pool.wait_ge(S[f"w_in{n % 2}"], 16 * (n // 2 + 1))
                    g.tensor_copy(hi, wraw[:, n % 2, 0:w]).then_inc(S["wb_hi"], 1)
                    pool.wait_ge(S["wb_hi"], n + 1)
                    g.tensor_tensor(lo, wraw[:, n % 2, 0:w], hi.bitcast(F32), ALU.subtract).then_inc(S["wb_lo"], 1)
            def power(n):
                pool.wait_ge(S["ln_eps"], n + 1)
                g.tensor_tensor(rstd[:, 0:4], rstd[:, 0:4], pw[:, 0:4], ALU.pow).then_inc(S["ln_pow"], 1)
            pieces_to(0, N_QK)
            for n in range(4):
                power(n)
            pieces_to(N_QK, N_V)
            piece_at = N_V
            for h in range(2):
                for kind in range(2):
                    pool.wait_ge(S["line_ok"], 2 * h + kind + 1)
                    if h == 1:
                        pool.wait_ge(S["a_mm"], 16)
                        pool.wait_ge(S["bd_ok"], 8)
                    g.tensor_copy(C[kind][:, 0], th[:, kind]).then_inc(S["c_hi"], 1)
                    pool.wait_ge(S["c_hi"], 2 * h + kind + 1)
                    g.tensor_tensor(C[kind][:, 1], th[:, kind], C[kind][:, 0].bitcast(F32), ALU.subtract).then_inc(S["c_lo"], 1)
                if h == 0:
                    pieces_to(N_V, N_O)
                for t in range(4 * h, 4 * h + 4):
                    for gq in range(4):
                        n = 4 * t + gq
                        pool.wait_ge(S["a_hi"], n + 1)
                        g.tensor_tensor(A[:, gq % 2, 1], At[:, gq % 2], A[:, gq % 2, 0].bitcast(F32), ALU.subtract).then_inc(S["a_lo"], 1)
            for n in range(4, 6):
                power(n)
            pool.wait_ge(S["b2_in"], 16)
            for t in range(T):
                if t % 4 == 0:
                    pool.wait_ge(S["ln_out"], 16 + t + 4)
                g.tensor_tensor(z[:, t], z[:, t], xs[:, t], ALU.add).then_inc(S["base_ok"], 1)
                pool.wait_ge(S["base_ok"], 2 * t + 1)
                g.tensor_tensor(z[:, t], z[:, t], b2_bc, ALU.add).then_inc(S["base_ok"], 1)
            for part in range(2):
                if part == 1:
                    for m in range(6, 8):
                        power(m)
                    pool.wait_ge(S["rw_in"], 32)
                    g.tensor_copy(rws[:, 0], rw_raw).then_inc(S["r_hi"], 1)
                    g.tensor_copy(e2s[0:32, 0], e2_raw[0:32]).then_inc(S["r_hi"], 1)
                    pool.wait_ge(S["r_hi"], 2)
                    g.tensor_tensor(rws[:, 1], rw_raw, rws[:, 0].bitcast(F32), ALU.subtract).then_inc(S["r_lo"], 1)
                    g.tensor_tensor(e2s[0:32, 1], e2_raw[0:32], e2s[0:32, 0].bitcast(F32), ALU.subtract).then_inc(S["r_lo"], 1)
        def act_tail(act):
            a = nc.scalar
            act.wait_ge(S["cols_in"], 7 * 16)

            def affine(h, base, w, b):
                for k in range(KD):
                    n = base + 4 * h + k
                    act.wait_ge(S["t_mm"], n + 1)
                    if n >= 2:
                        act.wait_ge(S["y_lo2"], n - 1)
                    if w is None:
                        a.copy(yF[:, k % 2], TR[k % 2][:]).then_inc(S["y_f"], 1)
                    else:
                        a.activation(yF[:, k % 2], TR[k % 2][:], ACT.Identity, bias=b[:, k:k + 1], scale=w[:, k:k + 1]).then_inc(S["y_f"], 1)
                    act.wait_ge(S["y_f"], n + 1)
                    if base == 0 and k == 0:
                        act.wait_ge(S["o_mm"], T)
                    if base == 8 and k == 0 and h == 0:
                        act.wait_ge(S["v2_mm"], 2 * T)
                        act.wait_ge(S["qk_mm"], 4)
                    if base == 16 and k == 0:
                        act.wait_ge(S["f_mm"], 16 * (h + 1))
                    a.copy(yT[h][:, 0, k], yF[:, k % 2]).then_inc(S["y_hi2"], 1)

            def angles(h):
                for kind in range(2):
                    act.wait_ge(S["qk_mm"], 2 * h + kind + 1)
                    if h == 1:
                        act.wait_ge(S["c_lo"], kind + 1)
                    a.activation(th[:, kind], SC[kind][:], ACT.Tanh).then_inc(S["th_ok"], 1)
                for kind in range(2):
                    act.wait_ge(S["th_ok"], 2 * h + kind + 1)
                    a.activation(th[:, kind], th[:, kind], ACT.Identity, bias=line[:, 2 * kind + 1:2 * kind + 2], scale=line[:, 2 * kind:2 * kind + 1]).then_inc(S["line_ok"], 1)

            def cosine(n):
                act.wait_ge(S["a_mm"], n + 1)
                if n >= 2:
                    act.wait_ge(S["a_lo"], n - 1)
                a.activation(At[:, n % 2], SC[n % 2][:], ACT.Abs).then_inc(S["abs_ok"], 1)
                act.wait_ge(S["abs_ok"], n + 1)
                a.activation(At[:, n % 2], At[:, n % 2], ACT.Sin, bias=quarter, scale=-1.0).then_inc(S["cos_ok"], 1)

            def a_high(n):
                act.wait_ge(S["a_ok"], n + 1)
                if n >= 2:
                    act.wait_ge(S["nd_mm"], n - 1)
                a.copy(A[:, n % 2, 0], At[:, n % 2]).then_inc(S["a_hi"], 1)

            def den_eps(n):
                act.wait_ge(S["nd_mm"], n + 1)
                if n >= 2:
                    act.wait_ge(S["h_lo"], 2 * (n - 1))
                a.activation(den[:, n % 2], pb[(4, 7)[n % 2]][:], ACT.Identity, bias=eps_c[:, 0:1]).then_inc(S["den_ok"], 1)

            act.wait_ge(S["eps_set"], 1)
            affine(0, 0, l1w, l1b)
            affine(1, 0, l1w, l1b)
            for h in range(2):
                angles(h)
                for t in range(4 * h, 4 * h + 4):
                    for n in range(2):
                        act.wait_ge(S["v2_mm"], 2 * t + n + 1)
                        if n == 0 and t > 0:
                            act.wait_ge(S["nd_mm"], 4 * t)
                        a.copy(v2[:, 0, n * 512:(n + 1) * 512], KV[n][:]).then_inc(S["v2_hi"], 1)
                    cosine(4 * t)
                    cosine(4 * t + 1)
                    a_high(4 * t)
                    a_high(4 * t + 1)
                    den_eps(4 * t)
                    cosine(4 * t + 2)
                    a_high(4 * t + 2)
                    den_eps(4 * t + 1)
                    cosine(4 * t + 3)
                    a_high(4 * t + 3)
                    den_eps(4 * t + 2)
                    den_eps(4 * t + 3)
            affine(0, 8, l2w, l2b)
            affine(1, 8, l2w, l2b)
            def w1_high(part, h, c, par):
                j = total(part, h)
                act.wait_ge(S[f"w1_in{par}"], (c + (j + 2 - par)) * 8)
                if isinstance(c, int) and j + c < 2:
                    act.wait_ge(S["v2_mm"], 2 * T)
                else:
                    act.wait_ge(S["hmm"], c + (j - 1))
                a.copy(w1c[:, par, 0], w1raw[:, par]).then_inc(S["w1_hi"], 1)

            def w2_high(part, h, c, par):
                j = total(part, h)
                act.wait_ge(S[f"w2_in{par}"], (c + (j + 2 - par)) * 8)
                if isinstance(c, int) and j + c < 2:
                    act.wait_ge(S["v2_mm"], 2 * T)
                else:
                    act.wait_ge(S["f_mm"], c + (j - 1))
                a.copy(w2c[:, par, 0], w2raw[:, par]).then_inc(S["w2_hi"], 1)

            def hidden(part, h, c, par):
                j, bias = total(part, h), parts[part][2]
                act.wait_ge(S["hmm"], c + (j + 1))
                if isinstance(c, int) and j + c == 0:
                    act.wait_ge(S["base_ok"], 2 * T)
                if not (isinstance(c, int) and j + c < 2):
                    act.wait_ge(S["hh_lo"], c + (j - 1))
                bias_c = bias[:, c:c + 1] if isinstance(c, int) else bias[:, bass.ds(c, 1)]
                a.activation(hF[:, par], pb[5 + par][:], ACT.Relu if part else ACT.Gelu_apprx_tanh, bias=bias_c).then_inc(S["hact"], 1)
            for part in range(2):
                if part == 1:
                    affine(0, 16, None, None)
                    affine(1, 16, None, None)
                for h in range(2):
                    weight_loop(act, part, h, hidden, w1_high, w2_high)

        def dve_tail(dve):
            d = nc.vector
            c_ln = [0, 0]
            d.memset(eps_c[:], 1e-6).then_inc(S["eps_set"], 1)
            d.memset(onesr[:].bitcast(F32), 1.0).then_inc(S["onesr_ok"], 1)

            def layernorm(h, src, dst):
                n, c = c_ln
                for t in range(4):
                    d.bn_stats(st[:, 6 * (t % 2):6 * (t % 2) + 6], src[:, 4 * h + t]).then_inc(S["ln_st"], 1)
                    dve.wait_ge(S["ln_st"], n + t + 1)
                    d.bn_aggr(mv[:, 2 * t:2 * t + 2], st[:, 6 * (t % 2):6 * (t % 2) + 6]).then_inc(S["ln_mv"], 1)
                dve.wait_ge(S["ln_mv"], n + 4)
                d.tensor_scalar(rstd[:, 0:4], mvv[:, 0:4, 1], EPS, None, ALU.add).then_inc(S["ln_eps"], 1)
                dve.wait_ge(S["ln_pow"], c + 1)
                for t in range(4):
                    d.tensor_scalar(dst[:, 4 * h + t], src[:, 4 * h + t], mv[:, 2 * t:2 * t + 1], rstd[:, t:t + 1],
                                    ALU.subtract, ALU.mult).then_inc(S["ln_out"], 1)
                c_ln[0], c_ln[1] = n + 4, c + 1
                dve.wait_ge(S["ln_out"], n + 4)

            def low(h, base):
                for k in range(KD):
                    n = base + 4 * h + k
                    dve.wait_ge(S["y_hi2"], n + 1)
                    d.tensor_tensor(yT[h][:, 1, k], yF[:, k % 2], yT[h][:, 0, k].bitcast(F32), ALU.subtract).then_inc(S["y_lo2"], 1)

            dve.wait_ge(S["xb_ok"], T)
            for h in range(2):
                for t in range(4 * h, 4 * h + 4):
                    dve.wait_ge(S["o_mm"], t + 1)
                    d.tensor_tensor(xs[:, t], pb[OB[t]][:], xs[:, t], ALU.add).then_inc(S["x1_ok"], 1)
                dve.wait_ge(S["x1_ok"], 4 * h + 4)
                if h == 0:
                    dve.wait_ge(S["aT_lo"], NB)
                layernorm(h, xs, z)
                layernorm(h, z, zn)
            low(0, 0)
            low(1, 0)

            def pair_masks(t):
                dve.wait_ge(S["c_lo"], 2 * (t // 4) + 2)
                if t > 0:
                    dve.wait_ge(S["a_mm"], 4 * t)
                tok = slice((t % 4) * P, (t % 4) * P + P)
                for s_ in range(2):
                    d.tensor_tensor(bd[:, s_].rearrange("p (i q) -> p i q", i=4),
                                    C[1][:, s_, tok].bitcast(F32).unsqueeze(1).to_broadcast([P, 4, P]),
                                    mask4.unsqueeze(2).to_broadcast([P, 4, P]), ALU.mult).then_inc(S["bd_ok"], 1)

            def a_mask(n):
                dve.wait_ge(S["cos_ok"], n + 1)
                d.tensor_tensor(At[:, n % 2].rearrange("p (i q) -> p i q", i=4), At[:, n % 2].rearrange("p (i q) -> p i q", i=4),
                                causal.unsqueeze(1).to_broadcast([P, 4, P]), ALU.mult).then_inc(S["a_ok"], 1)

            def heads(n):
                t, gq = n // 4, n % 4
                dve.wait_ge(S["den_ok"], n + 1)
                d.reciprocal(den[:, n % 2], den[:, n % 2]).then_inc(S["rec_ok"], 1)
                dve.wait_ge(S["rec_ok"], n + 1)
                if gq == 0 and t > 0:
                    dve.wait_ge(S["wo2_mm"], t)
                for i in range(2):
                    r = slice(64 * i, 64 * i + 64)
                    v4 = lambda ap: ap.rearrange("p (c i q) -> p c i q", c=2, i=2)[r, :, i]
                    d.tensor_tensor(v4(den[:, n % 2]), v4(TR[n % 2][:]), v4(den[:, n % 2]), ALU.mult).then_inc(S["h_f"], 1)
                dve.wait_ge(S["h_f"], 2 * n + 2)
                for i in range(2):
                    r = slice(64 * i, 64 * i + 64)
                    v4 = lambda ap: ap.rearrange("p (c i q) -> p c i q", c=2, i=2)[r, :, i]
                    d.tensor_copy(hT[r, 0, 2 * gq:2 * gq + 2], v4(den[:, n % 2])).then_inc(S["h_hi"], 1)
                dve.wait_ge(S["h_hi"], 2 * n + 2)
                for i in range(2):
                    r = slice(64 * i, 64 * i + 64)
                    v4 = lambda ap: ap.rearrange("p (c i q) -> p c i q", c=2, i=2)[r, :, i]
                    ins = d.tensor_tensor(hT[r, 1, 2 * gq:2 * gq + 2], v4(den[:, n % 2]), hT[r, 0, 2 * gq:2 * gq + 2].bitcast(F32), ALU.subtract)
                    ins.then_inc(S["h_lo"], 1)

            def z2(t):
                dve.wait_ge(S["wo2_mm"], t + 1)
                d.tensor_tensor(z[:, t], KV[0][:], z[:, t], ALU.add).then_inc(S["z2_ok"], 1)

            for t in range(T):
                pair_masks(t)
                for n in range(2):
                    dve.wait_ge(S["v2_hi"], 2 * t + n + 1)
                    d.tensor_tensor(v2[:, 1, n * 512:(n + 1) * 512], KV[n][:], v2[:, 0, n * 512:(n + 1) * 512].bitcast(F32), ALU.subtract).then_inc(S["v2_lo"], 1)
                a_mask(4 * t)
                a_mask(4 * t + 1)
                if t > 0:
                    z2(t - 1)
                heads(4 * t)
                a_mask(4 * t + 2)
                heads(4 * t + 1)
                a_mask(4 * t + 3)
                heads(4 * t + 2)
                heads(4 * t + 3)
            z2(T - 1)
            dve.wait_ge(S["z2_ok"], T)
            dve.wait_ge(S["a_lo"], 4 * T)
            layernorm(0, z, zn)
            layernorm(1, z, zn)
            low(0, 8)
            low(1, 8)
            for part, (_, _, _, n, before) in enumerate(parts):
                if part == 1:
                    layernorm(0, xs, zn)
                    layernorm(1, xs, zn)
                    low(0, 16)
                    low(1, 16)
                    for t in range(T):
                        dve.wait_ge(S["lg_mm"], t + 1)
                        s_ = t % 2
                        d.tensor_tensor(lg[:, 32 * s_:32 * s_ + 32], KV[s_][:, 0:32], rbs[:], ALU.add).then_inc(S["lg_ok"], 1)
                        dve.wait_ge(S["lg_ok"], t + 1)
                        d.max(top[:, 8 * s_:8 * s_ + 8], lg[:, 32 * s_:32 * s_ + 32]).then_inc(S["top_ok"], 1)
                        dve.wait_ge(S["top_ok"], t + 1)
                        d.max_index(topi[:, 8 * s_:8 * s_ + 8], top[:, 8 * s_:8 * s_ + 8], lg[:, 32 * s_:32 * s_ + 32]).then_inc(S["topi_ok"], 1)
                        dve.wait_ge(S["topi_ok"], t + 1)
                        d.tensor_copy(idf[:, s_:s_ + 1], topi[:, 8 * s_:8 * s_ + 1]).then_inc(S["id_ok"], 1)
                        dve.wait_ge(S["id_ok"], t + 1)
                        if t > 0:
                            dve.wait_ge(S["idx_mm"], t)
                        d.tensor_scalar(didx, ident, idf[:, s_:s_ + 1], None, ALU.mult).then_inc(S["di_ok"], 1)
                        dve.wait_ge(S["idx_mm"], t + 1)
                        d.tensor_copy(idx[:, t * P:(t + 1) * P], SC[0][:, 0:P]).then_inc(S["idx_ok"], 1)
                    dve.wait_ge(S["idx_ok"], T)
                    d.tensor_scalar(oneh, idx, cs[:, 2 * P + 39:2 * P + 40], None, ALU.is_equal).then_inc(S["one_ok"], 1)
                for h in range(2):
                    c0 = before + n * h

                    def w1_low(part, h, c, par):
                        dve.wait_ge(S["w1_hi"], c + (total(part, h) + 1))
                        d.tensor_tensor(w1c[:, par, 1], w1raw[:, par], w1c[:, par, 0].bitcast(F32), ALU.subtract).then_inc(S["w1_lo"], 1)

                    def w2_low(part, h, c, par):
                        dve.wait_ge(S["w2_hi"], c + (total(part, h) + 1))
                        d.tensor_tensor(w2c[:, par, 1], w2raw[:, par], w2c[:, par, 0].bitcast(F32), ALU.subtract).then_inc(S["w2_lo"], 1)

                    def hidden(part, h, c, par):
                        j = total(part, h)
                        dve.wait_ge(S["hact"], c + (j + 1))
                        if part == 1:
                            e_c = enum[:, c:c + 1] if isinstance(c, int) else enum[:, bass.ds(c, 1)]
                            d.scalar_tensor_tensor(out=hF[:, par], in0=idx[:, h * 512:(h + 1) * 512], scalar=e_c, in1=hF[:, par],
                                                   op0=ALU.is_equal, op1=ALU.mult).then_inc(S["hmask"], 1)
                            dve.wait_ge(S["hmask"], c + (n * h + 1))
                        if not (isinstance(c, int) and j + c < 2):
                            dve.wait_ge(S["f_mm"], c + (j - 1))
                        d.tensor_copy(hh[:, par, 0], hF[:, par]).then_inc(S["hh_hi"], 1)
                        dve.wait_ge(S["hh_hi"], c + (j + 1))
                        d.tensor_tensor(hh[:, par, 1], hF[:, par], hh[:, par, 0].bitcast(F32), ALU.subtract).then_inc(S["hh_lo"], 1)
                    weight_loop(dve, part, h, hidden, w1_low, w2_low)
                    if part == 0:
                        dve.wait_ge(S["f_mm"], c0 + n)
                        dve.wait_ge(S["base_ok"], 2 * T)
                        for t in range(4):
                            d.tensor_tensor(xs[:, 4 * h + t], pb[t][:], z[:, 4 * h + t], ALU.add).then_inc(S["x3_ok"], 1)
                        dve.wait_ge(S["x3_ok"], 4 * h + 4)
                    else:
                        dve.wait_ge(S["f_mm"], c0 + n)
                        for t in range(4 * h, 4 * h + 4):
                            d.scalar_tensor_tensor(out=xs[:, t], in0=pb[t % 4][:], scalar=0.0, in1=xs[:, t],
                                                   op0=ALU.max, op1=ALU.add).then_inc(S["fin_out1"], 1)

        def pe_tail(pe, mm3):
            pair = lambda f: [f(0), f(1)]

            def turn(h, base):
                for k in range(KD):
                    n = base + 4 * h + k
                    pe.wait_ge(S["ln_out"], {0: 8, 8: 20, 16: 28}[base] + (8 if base == 0 else 4) * h)
                    if n >= 2:
                        pe.wait_ge(S["y_lo2"], n - 1)
                    for t in range(4):
                        ins = nc.tensor.transpose(TR[k % 2][:, t * P:(t + 1) * P], zn[:, 4 * h + t, k * P:(k + 1) * P], ident)
                    ins.then_inc(S["t_mm"], 1)

            for t in range(T):
                pe.wait_ge(S["aT_lo"], 2 * t + 2)
                pe.wait_ge(S["wb_lo"], N_WO)
                if t == 0:
                    pe.wait_ge(S["pv_out"], 4 * NB)
                    pe.wait_ge(S["pv_out2"], 4 * NB)
                if t >= 5:
                    pe.wait_ge(S["x1_ok"], t - 4)
                for k in range(KD):
                    ins = mm3(pb[OB[t]][:], pair(lambda s_: aT[:, s_, k, t * P:(t + 1) * P]), pair(lambda s_: wo[:, s_, k]), k == 0, k == KD - 1)
                ins.then_inc(S["o_mm"], 1)
            pe.wait_ge(S["x1_ok"], T)
            turn(0, 0)
            turn(1, 0)
            pe.wait_ge(S["wb_lo"], N_V)
            pe.wait_ge(S["onesr_ok"], 1)
            for h in range(2):
                pe.wait_ge(S["y_lo2"], 4 * h + 4)
                if h == 1:
                    pe.wait_ge(S["a_ok"], 16)
                for kind in range(2):
                    for k in range(KD):
                        ins = mm3(SC[kind][:], pair(lambda s_: wQK[:, kind, s_, k]), pair(lambda s_: yT[h][:, s_, k]), k == 0, k == KD - 1)
                    ins.then_inc(S["qk_mm"], 1)
                for t in range(4 * h, 4 * h + 4):
                    tok = slice((t % 4) * P, (t % 4) * P + P)
                    for n in range(2):
                        if t > 0:
                            pe.wait_ge(S["v2_lo"], 2 * t - 2 + n + 1)
                        if t > 1 and n == 0:
                            pe.wait_ge(S["z2_ok"], t - 1)
                        for k in range(KD):
                            ins = mm3(KV[n][:], pair(lambda s_: yT[h][:, s_, k, tok]), pair(lambda s_: wV[:, s_, k, n * 512:(n + 1) * 512]), k == 0, k == KD - 1)
                        ins.then_inc(S["v2_mm"], 1)

                    def pairs_mm(gq):
                        n = 4 * t + gq
                        if gq == 0:
                            pe.wait_ge(S["bd_ok"], 2 * t + 2)
                            pe.wait_ge(S["line_ok"], 2 * h + 2)
                        if n >= 2:
                            pe.wait_ge(S["abs_ok"], n - 1)
                        r = slice(32 * gq, 32 * gq + 32)
                        mm3(SC[n % 2][:], pair(lambda s_: C[0][r, s_, tok]), pair(lambda s_: bd[r, s_]), True, True).then_inc(S["a_mm"], 1)

                    def weigh(gq):
                        n = 4 * t + gq
                        pe.wait_ge(S["a_lo"], n + 1)
                        if gq == 0:
                            pe.wait_ge(S["v2_lo"], 2 * t + 2)
                        if n >= 2:
                            pe.wait_ge(S["h_lo"], 2 * (n - 1))
                            pe.wait_ge(S["den_ok"], n - 1)
                        for c in range(2):
                            j = 2 * gq + c
                            w_ = pair(lambda s_: v2[:, s_, j * P:(j + 1) * P])
                            m_ = pair(lambda s_: A[:, n % 2, s_, c * 256:(c + 1) * 256])
                            dst = TR[n % 2][:, c * 256:(c + 1) * 256]
                            mm3(dst, w_, m_, True, True)
                        dd = pb[(4, 7)[n % 2]][:]
                        nc.tensor.matmul(dd, onesr[:], A[:, n % 2, 0], start=True, stop=False)
                        nc.tensor.matmul(dd, onesr[:], A[:, n % 2, 1], start=False, stop=True).then_inc(S["nd_mm"], 1)
                    def project(tt):
                        pe.wait_ge(S["h_lo"], 8 * (tt + 1))
                        pe.wait_ge(S["wb_lo"], N_O)
                        if tt == T - 1:
                            pe.wait_ge(S["v2_lo"], 2 * T)
                        for j in range(8):
                            ins = mm3(KV[0][:], pair(lambda s_: hT[:, s_, j]), pair(lambda s_: wO[:, s_, j]), j == 0, j == 7)
                        ins.then_inc(S["wo2_mm"], 1)
                    pairs_mm(0)
                    pairs_mm(1)
                    if t > 0:
                        pe.wait_ge(S["v2_lo"], 2 * t + 1)
                        project(t - 1)
                    weigh(0)
                    pairs_mm(2)
                    weigh(1)
                    pairs_mm(3)
                    weigh(2)
                    weigh(3)
            project(T - 1)
            turn(0, 8)
            turn(1, 8)
            for part, (_, _, _, n, before) in enumerate(parts):
                if part == 1:
                    turn(0, 16)
                    turn(1, 16)
                    pe.wait_ge(S["r_lo"], 2)
                    for t in range(T):
                        pe.wait_ge(S["y_lo2"], 16 + 4 * (t // 4) + 4)
                        tok = slice((t % 4) * P, (t % 4) * P + P)
                        if t >= 2:
                            pe.wait_ge(S["lg_ok"], t - 1)
                        for k in range(KD):
                            ins = mm3(KV[t % 2][:, 0:32], pair(lambda s_: yT[t // 4][:, s_, k, tok]), pair(lambda s_: rws[:, s_, k]), k == 0, k == KD - 1)
                        ins.then_inc(S["lg_mm"], 1)
                        pe.wait_ge(S["di_ok"], t + 1)
                        if t >= 1:
                            pe.wait_ge(S["idx_ok"], t)
                        nc.tensor.matmul(SC[0][:, 0:P], onesr[:], didx, start=True, stop=True).then_inc(S["idx_mm"], 1)
                for h in range(2):
                    c0 = before + n * h

                    def up(c, par):
                        pe.wait_ge(S["w1_lo"], c + (c0 + 1))
                        if isinstance(c, int) and c == 0:
                            pe.wait_ge(S["y_lo2"], (8 if part == 0 else 16) + 8)
                        if not (isinstance(c, int) and c0 + c < 2):
                            pe.wait_ge(S["hact"], c + (c0 - 1))
                        for k in range(KD):
                            ins = mm3(pb[5 + par][:], pair(lambda s_: w1c[:, par, s_, k * P:(k + 1) * P]), pair(lambda s_: yT[h][:, s_, k]), k == 0, k == KD - 1)
                        ins.then_inc(S["hmm"], 1)

                    def down(c, par, first, last):
                        pe.wait_ge(S["hh_lo"], c + (c0 + 1))
                        pe.wait_ge(S["w2_lo"], c + (c0 + 1))
                        for t in range(4):
                            ins = mm3(pb[t][:], pair(lambda s_: hh[:, par, s_, t * P:(t + 1) * P]), pair(lambda s_: w2c[:, par, s_]), first, last)
                        ins.then_inc(S["f_mm"], 1)

                    if part == 0 and h == 1:
                        pe.wait_ge(S["x3_ok"], 4)
                    if part == 1:
                        pe.wait_ge(S["one_ok"], 1)
                        if h == 1:
                            pe.wait_ge(S["fin_out1"], 4)
                        for t in range(4):
                            tt = slice((4 * h + t) * P, (4 * h + t + 1) * P)
                            nc.tensor.matmul(pb[t][:], oneh[0:32, tt], e2s[0:32, 0], start=True, stop=False)
                            nc.tensor.matmul(pb[t][:], oneh[0:32, tt], e2s[0:32, 1], start=False, stop=False)
                    up(0, 0)

                    def step(c, par):
                        if isinstance(c, int) and c == n - 1:
                            down(c, par, False, True)
                            return
                        up(c + 1, 1 - par)
                        down(c, par, part == 0 and isinstance(c, int) and c == 0, False)
                    chunk_loop(pe, n, step)

        def interleaved(key_step, T_, W_, O_):
            key_step(0)
            T_(0)
            T_(1)
            T_(2)
            W_(0)
            T_(3)
            W_(1)
            O_(0)
            key_step(1)
            T_(4)
            W_(2)
            T_(5)
            W_(3)
            O_(1)
            key_step(2)
            T_(6)
            W_(4)
            T_(7)
            W_(5)
            O_(2)
            key_step(3)
            W_(6)
            W_(7)
            O_(3)

        def nothing(*_):
            pass

        @block.sync
        def _(sp):
            for t in range(0, T, 2):
                sp.dma_start(xs[:, t:t + 2, :], x.rearrange("(t p) d -> p t d", p=P)[:, t:t + 2, :]).then_inc(S[f"x_in{t // 2}"], 16)
            sp.dma_start(cs[:], consts).then_inc(S["cs_in"], 16)
            sp.dma_start(bo_bc, bo.partition_broadcast(P)).then_inc(S["bo_in"], 16)
            for n, (dst, src) in enumerate(((l1w, ln1w), (l1b, ln1b), (l2w, ln2w), (l2b, ln2b), (b1s, b1), (e1s, e1))):
                sp.dma_start(dst, src).then_inc(S["cols_in"], 16)
            sp.dma_start(rbs[:], rb.partition_broadcast(P)).then_inc(S["cols_in"], 16)
            sp.dma_start(wq_raw, Wq.rearrange("(k p) n -> p k n", p=P)).then_inc(S["wq_in"], 16)
            for dst, src in ((bq_s, bq), (bk_s, bk), (bv_s, bv)):
                sp.dma_start(dst[:], src).then_inc(S["bias_in"], 16)
            sp.dma_start(wk_raw, Wk.rearrange("(k p) n -> p k n", p=P)).then_inc(S["wk_in"], 16)
            sp.dma_start(wv_raw, Wv.rearrange("(k p) n -> p k n", p=P)).then_inc(S["wv_in"], 16)

            def load(b, par):
                if not (isinstance(b, int) and b < 2):
                    sp.wait_ge(S["y_lo"], b - 1)
                sp.dma_start(yraw[:, par], ctxT.rearrange("b (k p) n -> b p k n", p=P)[bass.ds(b, 1)]
                             .rearrange("b p k n -> (b p) k n") if not isinstance(b, int) else
                             ctxT.rearrange("b (k p) n -> b p k n", p=P)[b]).then_inc(S[f"y_in{par}"], 16)
            load(0, 0)
            load(1, 1)
            with sp.Fori(0, LOOPS) as i:
                load(2 * i + 2, 0)
                load(2 * i + 3, 1)
            sp_tail(sp)

        @block.gpsimd
        def _(pool):
            g = nc.gpsimd
            g.memset(pw[:], -0.5).then_inc(S["ms_ok"], 1)
            pool.wait_ge(S["ms_ok"], 1)
            pool.wait_ge(S["cs_in"], 16)
            pool.wait_ge(S["eps_ok"], 1)
            g.tensor_tensor(rstd[:], rstd[:], pw[:], ALU.pow).then_inc(S["rstd_ok"], 1)
            pool.wait_ge(S["wq_in"], 16)
            g.tensor_copy(wq[:, 0], wq_raw).then_inc(S["wq_hi"], 1)
            pool.wait_ge(S["wq_hi"], 1)
            g.tensor_tensor(wq[:, 1], wq_raw, wq[:, 0].bitcast(F32), ALU.subtract).then_inc(S["wq_lo"], 1)
            pool.wait_ge(S["wk_in"], 16)
            pool.wait_ge(S["wv_in"], 16)
            g.tensor_copy(wk[:, 0], wk_raw).then_inc(S["wkv_hi"], 1)
            g.tensor_copy(wv[:, 0], wv_raw).then_inc(S["wkv_hi"], 1)
            pool.wait_ge(S["wkv_hi"], 2)
            g.tensor_tensor(wk[:, 1], wk_raw, wk[:, 0].bitcast(F32), ALU.subtract).then_inc(S["wkv_lo"], 1)
            g.tensor_tensor(wv[:, 1], wv_raw, wv[:, 0].bitcast(F32), ALU.subtract).then_inc(S["wkv_lo"], 1)

            def split_y(b, par):
                pool.wait_ge(S[f"y_in{par}"], ((b - par) // 2 + 1) * 16 if isinstance(b, int) else b * 8 + (16 - 8 * par))
                if not (isinstance(b, int) and b < 2):
                    pool.wait_ge(S["kv_mm"], 8 * b - 8)
                pool.nop(nofuse=True)
                g.tensor_copy(y[:, par, 0], yraw[:, par]).then_inc(S["y_hi"], 1)
                pool.wait_ge(S["y_hi"], b + 1)
                g.tensor_tensor(y[:, par, 1], yraw[:, par], y[:, par, 0].bitcast(F32), ALU.subtract).then_inc(S["y_lo"], 1)

            def normalise(b):
                for hg in range(HG):
                    pool.wait_ge(S["rs_ok"], 4 * b + hg + 1)
                    pool.nop(nofuse=True)
                    for hp in (2 * hg, 2 * hg + 1):
                        g.tensor_scalar(probs[:, hp], probs[:, hp], rs[:, hp:hp + 1], 1.0, ALU.mult, ALU.mult).then_inc(S["norm_ok"], 1)
            def split_out(b, par):
                pool.wait_ge(S["pv_out"], 4 * b + 4)
                pool.wait_ge(S["pv_out2"], 4 * b + 4)
                pool.nop(nofuse=True)
                cols_ = bass.ds(b * SQ, SQ)
                g.tensor_copy(aT[:, 0, :, cols_], attnT[:, par]).then_inc(S["aT_hi"], 1)
                pool.wait_ge(S["aT_hi"], b + 1)
                pool.nop(nofuse=True)
                g.tensor_tensor(aT[:, 1, :, cols_], attnT[:, par], aT[:, 0, :, cols_].bitcast(F32), ALU.subtract).then_inc(S["aT_lo"], 1)
            split_y(0, 0)
            pool.wait_ge(S["bo_in"], 16)
            pool.wait_ge(S["xn_ok"], T)
            for t in range(T):
                g.tensor_tensor(xs[:, t], xs[:, t], bo_bc, ALU.add).then_inc(S["xb_ok"], 1)
            split_y(1, 1)
            normalise(0)
            with pool.Fori(0, LOOPS) as i:
                split_y(2 * i + 2, 0)
                split_out(2 * i, 0)
                normalise(2 * i + 1)
                split_y(2 * i + 3, 1)
                split_out(2 * i + 1, 1)
                normalise(2 * i + 2)
            split_out(NB - 2, 0)
            normalise(NB - 1)
            split_out(NB - 1, 1)
            pool_tail(pool)

        @block.scalar
        def _(act):
            a = nc.scalar
            for t in range(T):
                act.wait_ge(S["xnT_mm"], t + 1)
                a.copy(xnT[:, 0, :, t * P:(t + 1) * P], TR[t % 2][:].rearrange("p (k n) -> p k n", k=KD)).then_inc(S["xnT_hi"], 1)

            def proj_hi(b, which, n):
                act.wait_ge(S["kv_mm"], 8 * b + 4 * which + n + 1)
                if which == 0:
                    if n == 0 and not (isinstance(b, int) and b == 0):
                        act.wait_ge(S["s_mm"], 8 * b)
                    a.activation(kT[:, 0, n], KV[n % 2][:], ACT.Identity, bias=bk_s[:, n:n + 1]).then_inc(S["kv_hi"], 1)
                else:
                    if n == 0 and not (isinstance(b, int) and b == 0):
                        act.wait_ge(S["pv_mm"], 4 * b)
                    a.copy(v[:, 0, n], KV[n % 2][:]).then_inc(S["kv_hi"], 1)

            def probs_hi(b, n):
                act.wait_ge(S["tr_mm"], 8 * b + n + 1)
                a.copy(pT[n % 4][:, 0], RING[n % 4][:]).then_inc(S["pT_hi"], 1)

            def out_evac(b, par, hg):
                if hg == 0 and not (isinstance(b, int) and b < 2):
                    act.wait_ge(S["aT_lo"], b - 1)
                act.wait_ge(S["pv_mm"], 4 * b + hg + 1)
                for j in range(2):
                    q = slice(32 * j, 32 * j + 32)
                    ins = a.activation(attnT[q, par, hg], PV[hg % 2][q, j * SQ:(j + 1) * SQ], ACT.Identity, bias=bv_s[q, hg:hg + 1])
                ins.then_inc(S["pv_out"], 1)

            def exps(b):
                for hp in range(8):
                    act.wait_ge(S["nmx_ok"], 8 * b + hp + 1)
                    if hp == 0 and not (isinstance(b, int) and b == 0):
                        act.wait_ge(S["tr_mm"], 8 * b)
                    a.activation(probs[:, hp], RING[hp % 4][:], ACT.Exp, bias=nmx[:, hp:hp + 1],
                                 accum_out=sums[:, hp:hp + 1]).then_inc(S["exp_ok"], 1)

            def body(b, par):
                first = isinstance(b, int) and b == 0
                act.wait_ge(S["bias_in"], 48) if first else None
                if first:
                    for n in range(4):
                        proj_hi(b, 0, n)
                else:
                    interleaved(lambda n: proj_hi(b, 0, n), lambda n: probs_hi(b - 1, n), nothing,
                                lambda hg: out_evac(b - 1, 1 - par, hg))
                for n in range(4):
                    proj_hi(b, 1, n)
                exps(b)
            over_batches(act, body)
            interleaved(nothing, lambda n: probs_hi(NB - 1, n), nothing, lambda hg: out_evac(NB - 1, 1, hg))
            act_tail(act)

        @block.vector
        def _(dve):
            d = nc.vector
            for t in range(T):
                dve.wait_ge(S[f"x_in{t // 2}"], 16)
                d.bn_stats(st[:, 6 * (t % 2):6 * (t % 2) + 6], xs[:, t]).then_inc(S["st_ok"], 1)
                dve.wait_ge(S["st_ok"], t + 1)
                d.bn_aggr(mv[:, 2 * t:2 * t + 2], st[:, 6 * (t % 2):6 * (t % 2) + 6]).then_inc(S["mv_ok"], 1)
            dve.wait_ge(S["mv_ok"], T)
            mvv = mv[:].rearrange("p (t c) -> p t c", c=2)
            d.tensor_scalar(rstd[:], mvv[:, :, 1], EPS, None, ALU.add).then_inc(S["eps_ok"], 1)
            dve.wait_ge(S["rstd_ok"], 1)

            def xnT_low(t):
                dve.wait_ge(S["xnT_hi"], t + 1)
                d.tensor_tensor(xnT[:, 1, :, t * P:(t + 1) * P], TR[t % 2][:].rearrange("p (k n) -> p k n", k=KD),
                                xnT[:, 0, :, t * P:(t + 1) * P].bitcast(F32), ALU.subtract).then_inc(S["xnT_lo"], 1)
            for t in range(T):
                if t >= 2:
                    dve.wait_ge(S["xnT_mm"], t - 1)
                d.tensor_scalar(xn[:, t % 2], xs[:, t], mv[:, 2 * t:2 * t + 1], rstd[:, t:t + 1],
                                ALU.subtract, ALU.mult).then_inc(S["xn_ok"], 1)
                if t >= 1:
                    xnT_low(t - 1)
            xnT_low(T - 1)
            dve.wait_ge(S["bias_in"], 48)
            dve.wait_ge(S["cs_in"], 16)
            dve.wait_ge(S["wkv_lo"], 2)
            for n in range(2 * HG):
                m, h = n % HG, n // HG
                dve.wait_ge(S["q_mm"], n + 1)
                d.tensor_scalar(qT[:, m, h * 512:(h + 1) * 512], KV[n % 2][:], bq_s[:, m:m + 1], SCALE,
                                ALU.add, ALU.mult).then_inc(S["q_ok"], 1)
            dve.wait_ge(S["q_ok"], 2 * HG)

            def proj_lo(b, which, n):
                dve.wait_ge(S["kv_hi"], 8 * b + 4 * which + n + 1)
                if which == 0:
                    d.scalar_tensor_tensor(out=kT[:, 1, n], in0=KV[n % 2][:], scalar=bk_s[:, n:n + 1],
                                           in1=kT[:, 0, n].bitcast(F32), op0=ALU.add, op1=ALU.subtract).then_inc(S["kv_lo"], 1)
                else:
                    d.tensor_tensor(v[:, 1, n], KV[n % 2][:], v[:, 0, n].bitcast(F32), ALU.subtract).then_inc(S["kv_lo"], 1)

            def spread_q(b, par):
                if not (isinstance(b, int) and b < 2):
                    dve.wait_ge(S["s_mm"], 8 * b - 8)
                src = qT[:, :, bass.ds(b * SQ, SQ)]
                for j in range(2):
                    d.tensor_scalar(qbd[:, par, 0, :, j * SQ:(j + 1) * SQ], src, half[:, j:j + 1], None, ALU.mult).then_inc(S["qbd_hi"], 1)
                for j in range(2):
                    dve.wait_ge(S["qbd_hi"], 2 * b + j + 1)
                    d.scalar_tensor_tensor(out=qbd[:, par, 1, :, j * SQ:(j + 1) * SQ], in0=src, scalar=half[:, j:j + 1],
                                           in1=qbd[:, par, 0, :, j * SQ:(j + 1) * SQ].bitcast(F32),
                                           op0=ALU.mult, op1=ALU.subtract).then_inc(S["qbd_ok"], 1)

            def probs_lo(b, n):
                dve.wait_ge(S["pT_hi"], 8 * b + n + 1)
                d.tensor_tensor(pT[n % 4][:, 1], RING[n % 4][:], pT[n % 4][:, 0].bitcast(F32), ALU.subtract).then_inc(S["pT_lo"], 1)

            def out_low_rows(b, par, hg):
                if hg == 0 and not (isinstance(b, int) and b < 2):
                    dve.wait_ge(S["aT_lo"], b - 1)
                dve.wait_ge(S["pv_mm"], 4 * b + hg + 1)
                for j in range(2, 4):
                    q = slice(32 * j, 32 * j + 32)
                    ins = d.tensor_scalar(attnT[q, par, hg], PV[hg % 2][q, j * SQ:(j + 1) * SQ], bv_s[q, hg:hg + 1], None, ALU.add)
                ins.then_inc(S["pv_out2"], 1)

            def maxima(b):
                for hp in range(8):
                    dve.wait_ge(S["s_mm"], 8 * b + hp + 1)
                    d.reduce_max(mx[:, hp:hp + 1], RING[hp % 4][:], AX).then_inc(S["mx_ok"], 1)
                    dve.wait_ge(S["mx_ok"], 8 * b + hp + 1)
                    d.tensor_scalar(nmx[:, hp:hp + 1], mx[:, hp:hp + 1], -1.0, None, ALU.mult).then_inc(S["nmx_ok"], 1)
                    if hp >= 2 and hp % 2 == 0:
                        reciprocals(b, hp // 2 - 1)
                reciprocals(b, 3)

            def reciprocals(b, hg):
                dve.wait_ge(S["exp_ok"], 8 * b + 2 * hg + 2)
                if not (isinstance(b, int) and b == 0) and hg == 0:
                    dve.wait_ge(S["norm_ok"], 8 * b)
                d.reciprocal(rs[:, 2 * hg:2 * hg + 2], sums[:, 2 * hg:2 * hg + 2]).then_inc(S["rs_ok"], 1)

            def body(b, par):
                if isinstance(b, int) and b == 0:
                    for n in range(4):
                        proj_lo(b, 0, n)
                else:
                    interleaved(lambda n: proj_lo(b, 0, n), lambda n: probs_lo(b - 1, n), nothing,
                                lambda hg: out_low_rows(b - 1, 1 - par, hg))
                spread_q(b, par)
                for n in range(4):
                    proj_lo(b, 1, n)
                maxima(b)
            over_batches(dve, body)
            interleaved(nothing, lambda n: probs_lo(NB - 1, n), nothing, lambda hg: out_low_rows(NB - 1, 1, hg))
            dve_tail(dve)

        @block.tensor
        def _(pe):
            def mm3(dst, w, m, first, last):
                nc.tensor.matmul(dst, w[1], m[0], start=first, stop=False)
                nc.tensor.matmul(dst, w[0], m[1], start=False, stop=False)
                return nc.tensor.matmul(dst, w[0], m[0], start=False, stop=last)

            pe.wait_ge(S["cs_in"], 16)
            for t in range(T):
                pe.wait_ge(S["xn_ok"], t + 1)
                if t >= 2:
                    pe.wait_ge(S["xnT_lo"], t - 1)
                for k in range(KD):
                    ins = nc.tensor.transpose(TR[t % 2][:, k * P:(k + 1) * P], xn[:, t % 2, k * P:(k + 1) * P], ident)
                ins.then_inc(S["xnT_mm"], 1)
            pe.wait_ge(S["wq_lo"], 1)
            for n in range(2 * HG):
                m, h = n % HG, n // HG
                pe.wait_ge(S["xnT_lo"], 4 * h + 4)
                if n >= 2:
                    pe.wait_ge(S["q_ok"], n - 1)
                for k in range(KD):
                    ins = mm3(KV[n % 2][:], [wq[:, s, k, m * P:(m + 1) * P] for s in range(2)],
                              [xnT[:, s, k, h * 512:(h + 1) * 512] for s in range(2)], k == 0, k == KD - 1)
                ins.then_inc(S["q_mm"], 1)
            pe.wait_ge(S["q_ok"], 2 * HG)
            pe.wait_ge(S["wkv_lo"], 2)

            def proj(b, par, which, n):
                if not (isinstance(b, int) and b == 0 and which == 0 and n < 2):
                    pe.wait_ge(S["kv_lo"], 8 * b + 4 * which + n - 1)
                if which == 0 and n == 0:
                    pe.wait_ge(S["y_lo"], b + 1)
                for k in range(KC):
                    ys = [y[:, par, s, k] for s in range(2)]
                    if which == 0:
                        ins = mm3(KV[n % 2][:], [wk[:, s, k, n * P:(n + 1) * P] for s in range(2)], ys, k == 0, k == KC - 1)
                    else:
                        ins = mm3(KV[n % 2][:], [z[:, n * P:(n + 1) * P] for z in ys], [wv[:, s, k] for s in range(2)],
                                  k == 0, k == KC - 1)
                ins.then_inc(S["kv_mm"], 1)

            def scores(b, par):
                pe.wait_ge(S["qbd_ok"], 2 * b + 2)
                for hp in range(8):
                    if hp < 4 and hp == 0:
                        pe.wait_ge(S["kv_lo"], 8 * b + 4)
                    if hp >= 4:
                        pe.wait_ge(S["exp_ok"], 8 * b + hp - 3)
                    elif not (isinstance(b, int) and b == 0):
                        pe.wait_ge(S["pT_lo"], 8 * b)
                    r = slice(64 * (hp % 2), 64 * (hp % 2) + 64)
                    mm3(RING[hp % 4][:], [qbd[r, par, s, hp // 2] for s in range(2)],
                        [kT[r, s, hp // 2] for s in range(2)], True, True).then_inc(S["s_mm"], 1)

            def transposes(b, n):
                hg = n // 2
                if n % 2 == 0:
                    pe.wait_ge(S["norm_ok"], 8 * b + 2 * hg + 2)
                if n < 4:
                    pe.wait_ge(S["exp_ok"], 8 * b + 5 + n)
                else:
                    pe.wait_ge(S["pT_lo"], 8 * b + n - 3)
                for c in range(2):
                    for j in range(2):
                        kc = 2 * (n % 2) + c
                        ins = nc.tensor.transpose(RING[n % 4][:, c * 256 + j * P:c * 256 + (j + 1) * P],
                                                  probs[:, 2 * hg + j, kc * P:(kc + 1) * P], ident)
                ins.then_inc(S["tr_mm"], 1)

            def weigh(b, n):
                hg = n // 2
                pe.wait_ge(S["pT_lo"], 8 * b + n + 1)
                if n % 2 == 0 and not (isinstance(b, int) and b == 0 and hg < 2):
                    pe.wait_ge(S["pv_out"], 4 * b + hg - 1)
                    pe.wait_ge(S["pv_out2"], 4 * b + hg - 1)
                for c in range(2):
                    kc = 2 * (n % 2) + c
                    ins = mm3(PV[hg % 2][:, 0:256], [v[:, s, kc, hg * P:(hg + 1) * P] for s in range(2)],
                              [pT[n % 4][:, s, c * 256:(c + 1) * 256] for s in range(2)], kc == 0, kc == 3)
                if n % 2 == 1:
                    ins.then_inc(S["pv_mm"], 1)

            def body(b, par):
                if isinstance(b, int) and b == 0:
                    for n in range(4):
                        proj(b, par, 0, n)
                else:
                    interleaved(lambda n: proj(b, par, 0, n), lambda n: transposes(b - 1, n), lambda n: weigh(b - 1, n), nothing)
                for n in range(4):
                    proj(b, par, 1, n)
                scores(b, par)
            over_batches(pe, body)
            interleaved(nothing, lambda n: transposes(NB - 1, n), lambda n: weigh(NB - 1, n), nothing)
            pe_tail(pe, mm3)


def layout(inputs):
    a = {n: np.asarray(v) for n, v in inputs.items()}
    P = 128
    X, T_ = "L0_xattn_", "L0_attn_"
    F_ = "L0_ffn_"
    c = np.ascontiguousarray
    cols = lambda v: c(v.reshape(-1, P).T)

    def spread(w, kinds):
        t = np.zeros((512, 4, 8, 4), np.float32)
        for r in range(kinds):
            t[:, :, r] = w[:, :, 0].T.reshape(512, 4, 4)
        return c(t.reshape(512, P))
    p = np.arange(P)
    consts = np.zeros((P, 2 * P + 44), np.float32)
    consts[:, 0:P] = np.eye(P)
    consts[:, P:2 * P] = (p[:, None] // 64 == p[None] // 64) & (p[:, None] <= p[None])
    consts[:, 2 * P:2 * P + 32] = np.arange(32)
    for j in range(2):
        consts[:, 2 * P + 32 + j] = (p // 32) % 2 == j
    for j in range(4):
        consts[:, 2 * P + 34 + j] = (p % 32 < 8) & (p % 4 == j)
    consts[:, 2 * P + 38] = np.pi / 2
    used, low = p % 32 < 8, p % 8 < 4
    consts[:, 2 * P + 40] = np.where(used & ~low, -np.pi / 4, 0)
    consts[:, 2 * P + 41] = used & low
    consts[:, 2 * P + 42] = np.where(used & low, np.pi / 4, 0)
    consts[:, 2 * P + 43] = used & ~low
    consts[:, 2 * P + 39] = p
    return {
        "x": c(a["x"].reshape(-1, 512)), "ctxT": c(a["ctx_768"].transpose(0, 2, 1)),
        "Wq": a[X + "Wq"], "bq": cols(a[X + "bq"]), "Wk": a[X + "Wk"], "bk": cols(a[X + "bk"]),
        "Wv": a[X + "Wv"], "bv": cols(a[X + "bv"]), "Wo": a[X + "Wo"], "bo": a[X + "bo"],
        "WQ": spread(a[T_ + "W_Q"], 2), "WK": spread(a[T_ + "W_K"], 2),
        "WV": c(a[T_ + "W_V"].transpose(1, 0, 2).reshape(512, 1024)),
        "WO": c(a[T_ + "W_O"].transpose(2, 1, 0).reshape(1024, 512)),
        "ln1w": cols(a[T_ + "ln1_w"]), "ln1b": cols(a[T_ + "ln1_b"]), "ln2w": cols(a[T_ + "ln2_w"]), "ln2b": cols(a[T_ + "ln2_b"]),
        "W1": a[T_ + "W1"], "b1": cols(a[T_ + "b1"]), "W2": a[T_ + "W2"], "b2": a[T_ + "b2"],
        "rw": c(a[F_ + "router_w"].T), "rb": a[F_ + "router_b"],
        "E1": a[F_ + "weights1"], "e1": c(a[F_ + "bias1"].T), "E2": a[F_ + "weights2"], "e2": a[F_ + "bias2"],
        "consts": consts,
    }


def kernel(**inputs):
    import concourse.bacc as bacc
    from concourse import mybir as _mybir
    from concourse.bass_utils import run_bass_kernel_spmd

    arrays = layout(inputs)
    nc = bacc.Bacc("TRN2", target_bir_lowering=False, num_devices=1)
    args = [nc.dram_tensor(n, a.shape, _mybir.dt.from_np(a.dtype), kind="ExternalInput").ap() for n, a in arrays.items()]
    args.append(nc.dram_tensor("out", (1024, 512), F32, kind="ExternalOutput").ap())
    build(nc, *args)
    r = run_bass_kernel_spmd(nc, [arrays], core_ids=[0])
    return r.results[0]["out"].reshape(16, 64, 512)
```

```python
import concourse.bass as bass
from concourse import mybir
from concourse.alu_op_type import AluOpType as ALU
import numpy as np

F32, F32R = mybir.dt.float32, mybir.dt.float32r
ACT = mybir.ActivationFunctionType
AX = mybir.AxisListType.X


def build(nc, x, ctxT, Wq, bq, Wk, bk, Wv, bv, Wo, bo, WQ, WK, WV, WO, ln1w, ln1b, ln2w, ln2b, W1, b1, W2, b2,
          rw, rb, E1, e1, E2, e2, consts, out, dbg=None):
    P = 128
    NB, SQ, D = 16, 64, 512
    SK, DC = ctxT.shape[2], ctxT.shape[1]
    T = NB * SQ // P
    KD, KC = D // P, DC // P
    NH, DH = 16, 32
    HG = D // P
    EPS = 1e-5
    SCALE = float(DH) ** -0.5

    from contextlib import ExitStack
    with ExitStack() as ctx:
        def sb(name, cols, dt=F32):
            return ctx.enter_context(nc.sbuf_tensor(name, [P, cols], dt))

        def ps(name):
            return ctx.enter_context(nc.psum_tensor(name, [P, 512], F32))

        def sem(name):
            return ctx.enter_context(nc.semaphore(name))

        R = sb("split_arena", 281 * 128, F32R)
        F = sb("plain_arena", 64 * 256, F32)

        def at(arena, kb, *shape):
            n = int(np.prod(shape))
            c = int(kb * 256)
            v = arena[:, c:c + n]
            if len(shape) == 1:
                return v
            names = "abcde"[:len(shape)]
            return v.rearrange(f"p ({' '.join(names)}) -> p {' '.join(names)}",
                               **{c: s for c, s in zip(names[1:], shape[1:])})

        wk = at(R, 0, 2, KC, D)
        wv = at(R, 12, 2, KC, D)
        y = at(R, 24, 2, 2, KC, SK)
        kT = at(R, 48, 2, HG, SK)
        v = at(R, 64, 2, SK // P, D)
        pT = [at(R, kb, 2, 512) for kb in (80, 84, 128, 132)]
        qbd = at(R, 88, 2, 2, HG, P)
        xnT = at(R, 48, 2, KD, T * P)
        wq = at(R, 80, 2, KD, D)

        aT = at(R, 96, 2, HG, T * P)

        xs = at(F, 0, T, D)
        qT = at(F, 16, HG, T * P)
        probs = at(F, 32, 8, SK)
        wq_raw = at(F, 32, KD, D)
        xn = at(F, 40, 2, D)
        yraw = at(F, 48, 2, KC, SK)
        wk_raw = at(F, 16, KC, D)
        wv_raw = at(F, 22, KC, D)
        bo_bc = at(F, 62, D)
        attnT = at(F, 60, 2, HG, SQ)

        wo = at(R, 0, 2, KD, D)
        yT = [at(R, 0, 2, KD, 512), at(R, 96, 2, KD, 512)]
        wV = at(R, 16, 2, KD, 1024)
        wO = at(R, 48, 2, 8, D)
        wQK = at(R, 80, 2, 2, KD, P)
        bd = at(R, 88, 2, 512)
        v2 = at(R, 112, 2, 16, 66)
        A = at(R, 120.5, 2, 2, 512)
        hT = at(R, 128.5, 2, 8, P)
        C = [at(R, 136.5, 2, 512), at(R, 92, 2, 512)]
        zn = at(F, 16, T, D)
        wraw = at(F, 32, 2, 1024)
        th = at(F, 40, 2, 512)
        yF = at(F, 44, 2, 512)
        hN = at(F, 24, 16, 64)
        wo_raw = at(F, 16, KD, D)
        qk_raw = at(F, 24, 2, KD, P)
        z = at(F, 48, T, D)
        At = at(F, 16, 4, 512)
        b2_bc = at(F, 42, D)

        w1c = at(R, 16, 2, 2, 512)
        w2c = at(R, 24, 2, 2, 512)
        hh = at(R, 32, 2, 2, 512)
        rws = at(R, 40, 2, KD, 32)
        e2s = at(R, 41, 2, D)
        oneh = at(R, 45, 1024)
        didx = at(R, 49, P)
        w1raw = at(F, 32, 2, 512)
        w2raw = at(F, 36, 2, 512)
        hF = at(F, 40, 2, 512)
        idx = at(F, 44, 1024)
        rw_raw = at(F, 50, KD, 32)
        e2_raw = at(F, 48, D)

        bq_s, bk_s, bv_s = sb("bq_s", HG), sb("bk_s", HG), sb("bv_s", HG)
        cs = sb("constants", consts.shape[1])
        ident, causal = cs[:, 0:P], cs[:, P:2 * P]
        o = 2 * P
        enum, half, mask4, line = cs[:, o:o + 32], cs[:, o + 32:o + 34], cs[:, o + 34:o + 38], cs[:, o + 40:o + 44]
        quarter = cs[:, o + 38:o + 39]
        onesr = ctx.enter_context(nc.sbuf_tensor("ones_r", [P, P], F32R))
        cols = sb("columns", 4 * KD + 16 + 32)
        l1w, l1b, l2w, l2b = (cols[:, 4 * i:4 * i + 4] for i in range(4))
        b1s, e1s = cols[:, 16:32], cols[:, 32:64]
        rbs = sb("rbs", 32)
        rden = sb("rden", 16)
        top, topi = sb("top8", 16), ctx.enter_context(nc.sbuf_tensor("top8i", [P, 16], mybir.dt.uint32))
        lg = sb("logits", 64)
        idf = sb("idf", 2)
        st, mv = sb("st", 6 * 2), sb("mv", 2 * T)
        mvv = mv[:].rearrange("p (t c) -> p t c", c=2)
        pw, rstd = sb("pw", T), sb("rstd", T)
        mx, nmx, sums, rs = sb("mx", 8), sb("nmx", 8), sb("sums", 8), sb("rs", 8)

        pb = [ps(f"bank{i}") for i in range(8)]
        KV, SC, TR = pb[0:2], pb[2:4], pb[5:7]
        RING = [pb[i] for i in (2, 3, 5, 6)]
        PV = [pb[4], pb[7]]
        AB = [pb[i] for i in (2, 3, 4, 7)]
        NUM = [pb[6], pb[5]]

        names = """x_in0 x_in1 x_in2 x_in3 wq_in wk_in wv_in bias_in  ms_ok st_ok mv_ok abs_ok cos_ok h_f eps_ok rstd_ok xn_ok xnT_mm
          xnT_hi xnT_lo q_mm q_ok wq_hi wq_lo wkv_hi wkv_lo wk_lo y_in0 y_in1 y_hi y_lo kv_mm kv_hi kv_lo
          qbd_hi qbd_ok s_mm mx_ok nmx_ok exp_ok rs_ok norm_ok cs_in bo_in cols_in aT_hi aT_lo xb_ok w_in0 w_in1 wb_hi wb_lo o_mm x1_ok ln_st ln_mv ln_eps ln_pow ln_out b2_in b2_ok t_mm y_f y_hi2 y_lo2 qk_mm th_ok line_ok c_hi c_lo v2_mm v2_hi v2_lo bd_ok a_mm a_ok a_hi a_lo nd_mm den_ok rec_ok v2_ones hT_mm wo_in wqk_in wo_hi wo_lo wqk_hi wqk_lo h_hi h_lo wo2_mm z2_ok base_ok w1_in0 w1_in1 w2_in0 w2_in1 w1_hi w1_lo w2_hi w2_lo hmm hact hmask hh_hi hh_lo f_mm x3_ok rw_in r_hi r_lo lg_mm lg_ok top_ok topi_ok id_ok di_ok idx_mm idx_ok one_ok onesr_ok fin_ok fin_out0 fin_out1 fin_in tr_mm pT_hi pT_lo pv_mm pv_out pv_out2 out_sem""".split()
        S = {n: sem(n) for n in names}
        block = ctx.enter_context(nc.Block())
        LOOPS = (NB - 2) // 2

        def over_batches(eng, body):
            body(0, 0)
            body(1, 1)
            with eng.Fori(0, LOOPS) as i:
                body(2 * i + 2, 0)
                body(2 * i + 3, 1)


        pieces = []
        for k in range(KD):
            pieces.append((WV[k * P:(k + 1) * P, :], [wV[:, s_, k] for s_ in range(2)], 1024))
        for k in range(8):
            pieces.append((WO[k * P:(k + 1) * P, :], [wO[:, s_, k] for s_ in range(2)], D))
        N_V, N_O = 4, 12
        OB = [0, 1, 2, 3, 4, 0, 1, 2]
        NT = [0, 1, 2, 3]
        parts = [(W1.rearrange("(k p) (c n) -> c p k n", p=P, n=P), W2.rearrange("(c p) n -> c p n", p=P), b1s, 16, 0),
                 (E1.rearrange("e (k p) n -> e p k n", p=P), E2, e1s, 32, 32)]

        def chunk_loop(eng, n, body):
            body(0, 0)
            with eng.Fori(0, (n - 2) // 2) as i:
                body(2 * i + 1, 1)
                body(2 * i + 2, 0)
            body(n - 1, 1)

        def source(w, c):
            return w[c] if isinstance(c, int) else w[bass.ds(c, 1)].rearrange(
                "c p k n -> (c p) k n" if len(w.shape) == 4 else "c p n -> (c p) n")

        def weight_loop(eng, part, h, hidden, split1, split2):
            n = parts[part][3]
            if part == 0 and h == 0:
                split1(part, 0, 0, 0)
                split1(part, 0, 1, 1)
                split2(part, 0, 0, 0)

            def step(c, par):
                hidden(part, h, c, par)
                split1(part, h, c + 2, par)
                split2(part, h, c + 1, 1 - par)
            step(0, 0)
            step(1, 1)
            with eng.Fori(1, (n - 2) // 2) as i:
                step(2 * i, 0)
                step(2 * i + 1, 1)
            nxt = {(0, 0): (0, 1), (0, 1): (1, 0), (1, 0): (1, 1), (1, 1): None}[part, h]
            hidden(part, h, n - 2, 0)
            if nxt:
                split1(*nxt, 0, 0)
            split2(part, h, n - 1, 1)
            hidden(part, h, n - 1, 1)
            if nxt:
                split1(*nxt, 1, 1)
                split2(*nxt, 0, 0)

        def total(part, h):
            return parts[part][4] + parts[part][3] * h

        def sp_tail(sp):
            for n, (src, _, w) in enumerate(pieces):
                if n == 0:
                    sp.wait_ge(S["qbd_ok"], 2 * NB)
                    sp.dma_start(wo_raw, Wo.rearrange("(k p) n -> p k n", p=P)).then_inc(S["wo_in"], 16)
                    for kind, W_ in enumerate((WK, WQ)):
                        sp.dma_start(qk_raw[:, kind], W_.rearrange("(k p) n -> p k n", p=P)).then_inc(S["wqk_in"], 16)
                if n < 2:
                    sp.wait_ge(S["tr_mm"], 8 * NB)
                else:
                    sp.wait_ge(S["wb_lo"], n - 1)
                sp.dma_start(wraw[:, n % 2, 0:w], src).then_inc(S[f"w_in{n % 2}"], 16)
            sp.wait_ge(S["a_lo"], 4 * T)
            sp.wait_ge(S["c_lo"], 4)
            sp.dma_start(b2_bc, b2.partition_broadcast(P)).then_inc(S["b2_in"], 16)
            def load1(part, h, c, par):
                j = total(part, h)
                if isinstance(c, int) and j + c < 2:
                    sp.wait_ge(S["wb_lo"], N_O)
                else:
                    sp.wait_ge(S["w1_lo"], c + (j - 1))
                sp.dma_start(w1raw[:, par].rearrange("p (k n) -> p k n", k=KD), source(parts[part][0], c)).then_inc(S[f"w1_in{par}"], 16)

            def load2(part, h, c, par):
                j = total(part, h)
                if not (isinstance(c, int) and j + c < 2):
                    sp.wait_ge(S["w2_lo"], c + (j - 1))
                sp.dma_start(w2raw[:, par], source(parts[part][1], c)).then_inc(S[f"w2_in{par}"], 16)
            for part in range(2):
                for h in range(2):
                    weight_loop(sp, part, h, lambda *_: None, load1, load2)
                    if part == 0 and h == 1:
                        sp.wait_ge(S["x3_ok"], T)
                        sp.dma_start(rw_raw, rw.rearrange("(k p) n -> p k n", p=P)).then_inc(S["rw_in"], 16)
                        sp.dma_start(e2_raw[0:32], e2).then_inc(S["rw_in"], 16)
            for t in range(T):
                sp.wait_ge(S["fin_out1"], t + 1)
                sp.dma_start(out.rearrange("(t p) d -> p t d", p=P)[:, t], xs[:, t]).then_inc(S["out_sem"], 16)
            sp.wait_ge(S["out_sem"], 16 * T)

        def pool_tail(pool):
            g = nc.gpsimd
            def pieces_to(a_, b_):
                for n in range(a_, b_):
                    _, (hi, lo), w = pieces[n]
                    pool.wait_ge(S["wb_hi"], n + 1)
                    g.tensor_tensor(lo, wraw[:, n % 2, 0:w], hi.bitcast(F32), ALU.subtract).then_inc(S["wb_lo"], 1)
            def power(n):
                pool.wait_ge(S["ln_eps"], n + 1)
                g.tensor_tensor(rstd[:, 0:4], rstd[:, 0:4], pw[:, 0:4], ALU.pow).then_inc(S["ln_pow"], 1)
            pieces_to(0, N_V)
            for n in range(4):
                power(n)
            for h in range(2):
                for kind in range(2):
                    pool.wait_ge(S["line_ok"], 2 * h + kind + 1)
                    if h == 1:
                        pool.wait_ge(S["a_mm"], 16)
                    g.tensor_copy(C[kind][:, 0], th[:, kind]).then_inc(S["c_hi"], 1)
                    pool.wait_ge(S["c_hi"], 2 * h + kind + 1)
                    g.tensor_tensor(C[kind][:, 1], th[:, kind], C[kind][:, 0].bitcast(F32), ALU.subtract).then_inc(S["c_lo"], 1)
                if h == 0:
                    pieces_to(N_V, N_O)
                for t in range(4 * h, 4 * h + 4):
                    for gq in range(4):
                        n = 4 * t + gq
                        pool.wait_ge(S["a_hi"], n + 1)
                        g.tensor_tensor(A[:, gq % 2, 1], At[:, gq], A[:, gq % 2, 0].bitcast(F32), ALU.subtract).then_inc(S["a_lo"], 1)
            for n in range(4, 6):
                power(n)
            pool.wait_ge(S["b2_in"], 16)
            for t in range(T):
                if t % 4 == 0:
                    pool.wait_ge(S["ln_out"], 16 + t + 4)
                g.tensor_tensor(z[:, t], z[:, t], xs[:, t], ALU.add).then_inc(S["base_ok"], 1)
                pool.wait_ge(S["base_ok"], 2 * t + 1)
                g.tensor_tensor(z[:, t], z[:, t], b2_bc, ALU.add).then_inc(S["base_ok"], 1)
            for part in range(2):
                if part == 1:
                    for m in range(6, 8):
                        power(m)
                    pool.wait_ge(S["rw_in"], 32)
                    g.tensor_copy(rws[:, 0], rw_raw).then_inc(S["r_hi"], 1)
                    g.tensor_copy(e2s[0:32, 0], e2_raw[0:32]).then_inc(S["r_hi"], 1)
                    pool.wait_ge(S["r_hi"], 2)
                    g.tensor_tensor(rws[:, 1], rw_raw, rws[:, 0].bitcast(F32), ALU.subtract).then_inc(S["r_lo"], 1)
                    g.tensor_tensor(e2s[0:32, 1], e2_raw[0:32], e2s[0:32, 0].bitcast(F32), ALU.subtract).then_inc(S["r_lo"], 1)
        def act_tail(act):
            a = nc.scalar
            act.wait_ge(S["cols_in"], 7 * 16)

            def affine(h, base, w, b):
                for k in range(KD):
                    n = base + 4 * h + k
                    act.wait_ge(S["t_mm"], n + 1)
                    if n >= 2:
                        act.wait_ge(S["y_lo2"], n - 1)
                    if w is None:
                        a.copy(yF[:, k % 2], TR[k % 2][:]).then_inc(S["y_f"], 1)
                    else:
                        a.activation(yF[:, k % 2], TR[k % 2][:], ACT.Identity, bias=b[:, k:k + 1], scale=w[:, k:k + 1]).then_inc(S["y_f"], 1)
                    act.wait_ge(S["y_f"], n + 1)
                    if base == 0 and k == 0:
                        act.wait_ge(S["o_mm"], T)
                    if base == 8 and k == 0 and h == 0:
                        act.wait_ge(S["v2_mm"], 2 * T)
                        act.wait_ge(S["qk_mm"], 4)
                    if base == 16 and k == 0:
                        act.wait_ge(S["f_mm"], 16 * (h + 1))
                    a.copy(yT[h][:, 0, k], yF[:, k % 2]).then_inc(S["y_hi2"], 1)

            def angles(h):
                for kind in range(2):
                    act.wait_ge(S["qk_mm"], 2 * h + kind + 1)
                    if h == 1:
                        act.wait_ge(S["c_lo"], kind + 1)
                    a.activation(th[:, kind], SC[kind][:], ACT.Tanh).then_inc(S["th_ok"], 1)
                for kind in range(2):
                    act.wait_ge(S["th_ok"], 2 * h + kind + 1)
                    a.activation(th[:, kind], th[:, kind], ACT.Identity, bias=line[:, 2 * kind + 1:2 * kind + 2], scale=line[:, 2 * kind:2 * kind + 1]).then_inc(S["line_ok"], 1)

            def cosine(n):
                act.wait_ge(S["a_mm"], n + 1)
                if n >= 4:
                    act.wait_ge(S["a_lo"], n - 3)
                a.activation(At[:, n % 4], AB[n % 4][:], ACT.Abs).then_inc(S["abs_ok"], 1)
                act.wait_ge(S["abs_ok"], n + 1)
                a.activation(At[:, n % 4], At[:, n % 4], ACT.Sin, bias=quarter, scale=-1.0).then_inc(S["cos_ok"], 1)

            def a_high(n):
                act.wait_ge(S["a_ok"], n + 1)
                if n >= 2:
                    act.wait_ge(S["nd_mm"], n - 1)
                a.copy(A[:, n % 2, 0], At[:, n % 4]).then_inc(S["a_hi"], 1)

            def v_high(t):
                for n in range(2):
                    act.wait_ge(S["v2_mm"], 2 * t + n + 1)
                    act.wait_ge(S["nd_mm"], 4 * t) if t > 0 else act.wait_ge(S["v2_ones"], 2)
                    a.copy(v2[:, 0, 8 * n:8 * n + 8, 0:64], KV[n][:].rearrange("p (i d) -> p i d", d=64)).then_inc(S["v2_hi"], 1)

            def weight_pieces(a_, b_):
                for n in range(a_, b_):
                    _, (hi, lo), w = pieces[n]
                    act.wait_ge(S[f"w_in{n % 2}"], 16 * (n // 2 + 1))
                    a.copy(hi, wraw[:, n % 2, 0:w]).then_inc(S["wb_hi"], 1)

            act.wait_ge(S["wo_in"], 16)
            act.wait_ge(S["kv_mm"], 8 * NB)
            a.copy(wo[:, 0], wo_raw).then_inc(S["wo_hi"], 1)
            act.wait_ge(S["wqk_in"], 32)
            act.wait_ge(S["pv_mm"], 4 * NB)
            for kind in range(2):
                a.copy(wQK[:, kind, 0], qk_raw[:, kind]).then_inc(S["wqk_hi"], 1)
            weight_pieces(0, N_V)
            affine(0, 0, l1w, l1b)
            affine(1, 0, l1w, l1b)
            v_high(0)
            for h in range(2):
                angles(h)
                if h == 0:
                    weight_pieces(N_V, N_O)
                for t in range(4 * h, 4 * h + 4):
                    cosine(4 * t)
                    cosine(4 * t + 1)
                    a_high(4 * t)
                    cosine(4 * t + 2)
                    a_high(4 * t + 1)
                    cosine(4 * t + 3)
                    a_high(4 * t + 2)
                    a_high(4 * t + 3)
                    if t + 1 < T:
                        v_high(t + 1)
                    for n in range(2):
                        act.wait_ge(S["hT_mm"], 2 * t + n + 1)
                        if n == 0 and t > 0:
                            act.wait_ge(S["wo2_mm"], t)
                        a.copy(hT[:, 0, 4 * n:4 * n + 4], SC[n][:].rearrange("p (c q) -> p c q", c=4)).then_inc(S["h_hi"], 1)
            affine(0, 8, l2w, l2b)
            affine(1, 8, l2w, l2b)
            def w1_high(part, h, c, par):
                j = total(part, h)
                act.wait_ge(S[f"w1_in{par}"], (c + (j + 2 - par)) * 8)
                if isinstance(c, int) and j + c < 2:
                    act.wait_ge(S["v2_mm"], 2 * T)
                else:
                    act.wait_ge(S["hmm"], c + (j - 1))
                a.copy(w1c[:, par, 0], w1raw[:, par]).then_inc(S["w1_hi"], 1)

            def w2_high(part, h, c, par):
                j = total(part, h)
                act.wait_ge(S[f"w2_in{par}"], (c + (j + 2 - par)) * 8)
                if isinstance(c, int) and j + c < 2:
                    act.wait_ge(S["v2_mm"], 2 * T)
                else:
                    act.wait_ge(S["f_mm"], c + (j - 1))
                a.copy(w2c[:, par, 0], w2raw[:, par]).then_inc(S["w2_hi"], 1)

            def hidden(part, h, c, par):
                j, bias = total(part, h), parts[part][2]
                act.wait_ge(S["hmm"], c + (j + 1))
                if isinstance(c, int) and j + c == 0:
                    act.wait_ge(S["base_ok"], 2 * T)
                if not (isinstance(c, int) and j + c < 2):
                    act.wait_ge(S["hh_lo"], c + (j - 1))
                bias_c = bias[:, c:c + 1] if isinstance(c, int) else bias[:, bass.ds(c, 1)]
                a.activation(hF[:, par], pb[5 + par][:], ACT.Relu if part else ACT.Gelu_apprx_tanh, bias=bias_c).then_inc(S["hact"], 1)
            for part in range(2):
                if part == 1:
                    affine(0, 16, None, None)
                    affine(1, 16, None, None)
                for h in range(2):
                    weight_loop(act, part, h, hidden, w1_high, w2_high)

        def dve_tail(dve):
            d = nc.vector
            c_ln = [0, 0]
            d.memset(onesr[:].bitcast(F32), 1.0).then_inc(S["onesr_ok"], 1)

            def layernorm(h, src, dst):
                n, c = c_ln
                for t in range(4):
                    d.bn_stats(st[:, 6 * (t % 2):6 * (t % 2) + 6], src[:, 4 * h + t]).then_inc(S["ln_st"], 1)
                    dve.wait_ge(S["ln_st"], n + t + 1)
                    d.bn_aggr(mv[:, 2 * t:2 * t + 2], st[:, 6 * (t % 2):6 * (t % 2) + 6]).then_inc(S["ln_mv"], 1)
                dve.wait_ge(S["ln_mv"], n + 4)
                d.tensor_scalar(rstd[:, 0:4], mvv[:, 0:4, 1], EPS, None, ALU.add).then_inc(S["ln_eps"], 1)
                dve.wait_ge(S["ln_pow"], c + 1)
                for t in range(4):
                    d.tensor_scalar(dst[:, 4 * h + t], src[:, 4 * h + t], mv[:, 2 * t:2 * t + 1], rstd[:, t:t + 1],
                                    ALU.subtract, ALU.mult).then_inc(S["ln_out"], 1)
                c_ln[0], c_ln[1] = n + 4, c + 1
                dve.wait_ge(S["ln_out"], n + 4)

            def low(h, base):
                for k in range(KD):
                    n = base + 4 * h + k
                    dve.wait_ge(S["y_hi2"], n + 1)
                    d.tensor_tensor(yT[h][:, 1, k], yF[:, k % 2], yT[h][:, 0, k].bitcast(F32), ALU.subtract).then_inc(S["y_lo2"], 1)

            dve.wait_ge(S["xb_ok"], T)
            dve.wait_ge(S["wo_hi"], 1)
            d.tensor_tensor(wo[:, 1], wo_raw, wo[:, 0].bitcast(F32), ALU.subtract).then_inc(S["wo_lo"], 1)
            dve.wait_ge(S["wqk_hi"], 2)
            for kind in range(2):
                d.tensor_tensor(wQK[:, kind, 1], qk_raw[:, kind], wQK[:, kind, 0].bitcast(F32), ALU.subtract).then_inc(S["wqk_lo"], 1)
            dve.wait_ge(S["wo_lo"], 1)
            dve.wait_ge(S["wqk_lo"], 2)
            for h in range(2):
                for t in range(4 * h, 4 * h + 4):
                    dve.wait_ge(S["o_mm"], t + 1)
                    d.tensor_tensor(xs[:, t], pb[OB[t]][:], xs[:, t], ALU.add).then_inc(S["x1_ok"], 1)
                dve.wait_ge(S["x1_ok"], 4 * h + 4)
                if h == 0:
                    dve.wait_ge(S["aT_lo"], NB)
                layernorm(h, xs, z)
                layernorm(h, z, zn)
            for s_ in range(2):
                d.memset(v2[:, s_, :, 64:66].bitcast(F32), 1.0 - s_).then_inc(S["v2_ones"], 1)
            low(0, 0)
            low(1, 0)

            def pair_masks(t):
                dve.wait_ge(S["c_lo"], 2 * (t // 4) + 2)
                if t > 0:
                    dve.wait_ge(S["a_mm"], 4 * t)
                tok = slice((t % 4) * P, (t % 4) * P + P)
                for s_ in range(2):
                    d.tensor_tensor(bd[:, s_].rearrange("p (i q) -> p i q", i=4),
                                    C[1][:, s_, tok].bitcast(F32).unsqueeze(1).to_broadcast([P, 4, P]),
                                    mask4.unsqueeze(2).to_broadcast([P, 4, P]), ALU.mult).then_inc(S["bd_ok"], 1)

            def a_mask(n):
                dve.wait_ge(S["cos_ok"], n + 1)
                ap = At[:, n % 4].rearrange("p (i q) -> p i q", i=4)
                d.tensor_tensor(ap, ap, causal.unsqueeze(1).to_broadcast([P, 4, P]), ALU.mult).then_inc(S["a_ok"], 1)

            def heads(n):
                t, gq = n // 4, n % 4
                dve.wait_ge(S["nd_mm"], n + 1)
                src = NUM[n % 2][:, 0:264].rearrange("p (i d) -> p i d", d=66)
                rd = rden[:, 4 * gq:4 * gq + 4]
                d.tensor_scalar(rd, src[:, :, 64], 1e-6, None, ALU.add).then_inc(S["den_ok"], 1)
                dve.wait_ge(S["den_ok"], n + 1)
                d.reciprocal(rd, rd).then_inc(S["rec_ok"], 1)
                dve.wait_ge(S["rec_ok"], n + 1)
                if gq == 0 and t > 0:
                    dve.wait_ge(S["hT_mm"], 2 * t)
                d.tensor_tensor(hN[:, 4 * gq:4 * gq + 4], src[:, :, 0:64], rd.unsqueeze(2).to_broadcast([P, 4, 64]), ALU.mult).then_inc(S["h_f"], 1)

            def v_low(t):
                for n in range(2):
                    dve.wait_ge(S["v2_hi"], 2 * t + n + 1)
                    d.tensor_tensor(v2[:, 1, 8 * n:8 * n + 8, 0:64], KV[n][:].rearrange("p (i d) -> p i d", d=64),
                                    v2[:, 0, 8 * n:8 * n + 8, 0:64].bitcast(F32), ALU.subtract).then_inc(S["v2_lo"], 1)

            def z2(t):
                dve.wait_ge(S["wo2_mm"], t + 1)
                d.tensor_tensor(z[:, t], NUM[1][:], z[:, t], ALU.add).then_inc(S["z2_ok"], 1)

            v_low(0)
            pair_masks(0)
            for t in range(T):
                for gq in range(4):
                    a_mask(4 * t + gq)
                if t > 0:
                    z2(t - 1)
                for gq in range(4):
                    heads(4 * t + gq)
                if t + 1 < T:
                    v_low(t + 1)
                for n in range(2):
                    dve.wait_ge(S["h_hi"], 2 * t + n + 1)
                    d.tensor_tensor(hT[:, 1, 4 * n:4 * n + 4], SC[n][:].rearrange("p (c q) -> p c q", c=4),
                                    hT[:, 0, 4 * n:4 * n + 4].bitcast(F32), ALU.subtract).then_inc(S["h_lo"], 1)
                if t + 1 < T:
                    pair_masks(t + 1)
            z2(T - 1)
            dve.wait_ge(S["z2_ok"], T)
            dve.wait_ge(S["a_lo"], 4 * T)
            layernorm(0, z, zn)
            layernorm(1, z, zn)
            low(0, 8)
            low(1, 8)
            for part, (_, _, _, n, before) in enumerate(parts):
                if part == 1:
                    layernorm(0, xs, zn)
                    layernorm(1, xs, zn)
                    low(0, 16)
                    low(1, 16)
                    for t in range(T):
                        dve.wait_ge(S["lg_mm"], t + 1)
                        s_ = t % 2
                        d.tensor_tensor(lg[:, 32 * s_:32 * s_ + 32], KV[s_][:, 0:32], rbs[:], ALU.add).then_inc(S["lg_ok"], 1)
                        dve.wait_ge(S["lg_ok"], t + 1)
                        d.max(top[:, 8 * s_:8 * s_ + 8], lg[:, 32 * s_:32 * s_ + 32]).then_inc(S["top_ok"], 1)
                        dve.wait_ge(S["top_ok"], t + 1)
                        d.max_index(topi[:, 8 * s_:8 * s_ + 8], top[:, 8 * s_:8 * s_ + 8], lg[:, 32 * s_:32 * s_ + 32]).then_inc(S["topi_ok"], 1)
                        dve.wait_ge(S["topi_ok"], t + 1)
                        d.tensor_copy(idf[:, s_:s_ + 1], topi[:, 8 * s_:8 * s_ + 1]).then_inc(S["id_ok"], 1)
                        dve.wait_ge(S["id_ok"], t + 1)
                        if t > 0:
                            dve.wait_ge(S["idx_mm"], t)
                        d.tensor_scalar(didx, ident, idf[:, s_:s_ + 1], None, ALU.mult).then_inc(S["di_ok"], 1)
                        dve.wait_ge(S["idx_mm"], t + 1)
                        d.tensor_copy(idx[:, t * P:(t + 1) * P], SC[0][:, 0:P]).then_inc(S["idx_ok"], 1)
                    dve.wait_ge(S["idx_ok"], T)
                    d.tensor_scalar(oneh, idx, cs[:, 2 * P + 39:2 * P + 40], None, ALU.is_equal).then_inc(S["one_ok"], 1)
                for h in range(2):
                    c0 = before + n * h

                    def w1_low(part, h, c, par):
                        dve.wait_ge(S["w1_hi"], c + (total(part, h) + 1))
                        d.tensor_tensor(w1c[:, par, 1], w1raw[:, par], w1c[:, par, 0].bitcast(F32), ALU.subtract).then_inc(S["w1_lo"], 1)

                    def w2_low(part, h, c, par):
                        dve.wait_ge(S["w2_hi"], c + (total(part, h) + 1))
                        d.tensor_tensor(w2c[:, par, 1], w2raw[:, par], w2c[:, par, 0].bitcast(F32), ALU.subtract).then_inc(S["w2_lo"], 1)

                    def hidden(part, h, c, par):
                        j = total(part, h)
                        dve.wait_ge(S["hact"], c + (j + 1))
                        if part == 1:
                            e_c = enum[:, c:c + 1] if isinstance(c, int) else enum[:, bass.ds(c, 1)]
                            d.scalar_tensor_tensor(out=hF[:, par], in0=idx[:, h * 512:(h + 1) * 512], scalar=e_c, in1=hF[:, par],
                                                   op0=ALU.is_equal, op1=ALU.mult).then_inc(S["hmask"], 1)
                            dve.wait_ge(S["hmask"], c + (n * h + 1))
                        if not (isinstance(c, int) and j + c < 2):
                            dve.wait_ge(S["f_mm"], c + (j - 1))
                        d.tensor_copy(hh[:, par, 0], hF[:, par]).then_inc(S["hh_hi"], 1)
                        dve.wait_ge(S["hh_hi"], c + (j + 1))
                        d.tensor_tensor(hh[:, par, 1], hF[:, par], hh[:, par, 0].bitcast(F32), ALU.subtract).then_inc(S["hh_lo"], 1)
                    weight_loop(dve, part, h, hidden, w1_low, w2_low)
                    if part == 0:
                        dve.wait_ge(S["f_mm"], c0 + n)
                        dve.wait_ge(S["base_ok"], 2 * T)
                        for t in range(4):
                            d.tensor_tensor(xs[:, 4 * h + t], pb[t][:], z[:, 4 * h + t], ALU.add).then_inc(S["x3_ok"], 1)
                        dve.wait_ge(S["x3_ok"], 4 * h + 4)
                    else:
                        dve.wait_ge(S["f_mm"], c0 + n)
                        for t in range(4 * h, 4 * h + 4):
                            d.scalar_tensor_tensor(out=xs[:, t], in0=pb[t % 4][:], scalar=0.0, in1=xs[:, t],
                                                   op0=ALU.max, op1=ALU.add).then_inc(S["fin_out1"], 1)

        def pe_tail(pe, mm3):
            pair = lambda f: [f(0), f(1)]

            def turn(h, base):
                for k in range(KD):
                    n = base + 4 * h + k
                    pe.wait_ge(S["ln_out"], {0: 8, 8: 20, 16: 28}[base] + (8 if base == 0 else 4) * h)
                    if n >= 2:
                        pe.wait_ge(S["y_lo2"], n - 1)
                    for t in range(4):
                        ins = nc.tensor.transpose(TR[k % 2][:, t * P:(t + 1) * P], zn[:, 4 * h + t, k * P:(k + 1) * P], ident)
                    ins.then_inc(S["t_mm"], 1)

            for t in range(T):
                pe.wait_ge(S["aT_lo"], 2 * t + 2)
                pe.wait_ge(S["wo_lo"], 1)
                if t == 0:
                    pe.wait_ge(S["pv_out"], 4 * NB)
                    pe.wait_ge(S["pv_out2"], 4 * NB)
                if t >= 5:
                    pe.wait_ge(S["x1_ok"], t - 4)
                for k in range(KD):
                    ins = mm3(pb[OB[t]][:], pair(lambda s_: aT[:, s_, k, t * P:(t + 1) * P]), pair(lambda s_: wo[:, s_, k]), k == 0, k == KD - 1)
                ins.then_inc(S["o_mm"], 1)
            pe.wait_ge(S["x1_ok"], T)
            turn(0, 0)
            turn(1, 0)
            pe.wait_ge(S["onesr_ok"], 1)

            def values(t):
                tok, h = slice((t % 4) * P, (t % 4) * P + P), t // 4
                if t == 0:
                    pe.wait_ge(S["wb_lo"], N_V)
                for n in range(2):
                    pe.wait_ge(S["y_lo2"], 4 * h + 4)
                    if t > 0:
                        pe.wait_ge(S["v2_lo"], 2 * t - 2 + n + 1)
                    for k in range(KD):
                        ins = mm3(KV[n][:], pair(lambda s_: yT[h][:, s_, k, tok]), pair(lambda s_: wV[:, s_, k, n * 512:(n + 1) * 512]), k == 0, k == KD - 1)
                    ins.then_inc(S["v2_mm"], 1)

            def angles(t, gq):
                n, tok = 4 * t + gq, slice((t % 4) * P, (t % 4) * P + P)
                if gq == 0:
                    pe.wait_ge(S["bd_ok"], 2 * t + 2)
                    if t > 0:
                        pe.wait_ge(S["h_lo"], 2 * t)
                if n >= 4:
                    pe.wait_ge(S["abs_ok"], n - 3)
                r = slice(32 * gq, 32 * gq + 32)
                mm3(AB[gq][:], pair(lambda s_: C[0][r, s_, tok]), pair(lambda s_: bd[r, s_]), True, True).then_inc(S["a_mm"], 1)

            def weigh(t, gq):
                n = 4 * t + gq
                pe.wait_ge(S["a_lo"], n + 1)
                if gq == 0:
                    pe.wait_ge(S["v2_lo"], 2 * t + 2)
                if n >= 2:
                    pe.wait_ge(S["h_f"], n - 1)
                if gq == 1 and t > 0:
                    pe.wait_ge(S["z2_ok"], t)
                for i in range(4):
                    ins = mm3(NUM[n % 2][:, 66 * i:66 * i + 66], pair(lambda s_: A[:, n % 2, s_, i * P:(i + 1) * P]),
                              pair(lambda s_: v2[:, s_, 4 * gq + i]), True, True)
                ins.then_inc(S["nd_mm"], 1)

            def turn_heads(t):
                pe.wait_ge(S["h_f"], 4 * t + 4)
                pe.wait_ge(S["abs_ok"], 4 * t + 2)
                hv = hN.rearrange("p (c i) d -> p c (i d)", i=2)
                for n in range(2):
                    for c in range(4):
                        ins = nc.tensor.transpose(SC[n][:, c * P:(c + 1) * P], hv[:, 4 * n + c], ident)
                    ins.then_inc(S["hT_mm"], 1)

            def project(t):
                pe.wait_ge(S["h_lo"], 2 * t + 2)
                pe.wait_ge(S["wb_lo"], N_O)
                pe.wait_ge(S["h_f"], 4 * t + 4)
                for j in range(8):
                    ins = mm3(NUM[1][:], pair(lambda s_: hT[:, s_, j]), pair(lambda s_: wO[:, s_, j]), j == 0, j == 7)
                ins.then_inc(S["wo2_mm"], 1)

            values(0)
            pe.wait_ge(S["wqk_lo"], 2)
            for h in range(2):
                pe.wait_ge(S["y_lo2"], 4 * h + 4)
                if h == 1:
                    pe.wait_ge(S["h_lo"], 8)
                for kind in range(2):
                    for k in range(KD):
                        ins = mm3(SC[kind][:], pair(lambda s_: wQK[:, kind, s_, k]), pair(lambda s_: yT[h][:, s_, k]), k == 0, k == KD - 1)
                    ins.then_inc(S["qk_mm"], 1)
                pe.wait_ge(S["th_ok"], 2 * h + 2)
                for t in range(4 * h, 4 * h + 4):
                    for gq in range(4):
                        angles(t, gq)
                    if t > 0:
                        project(t - 1)
                    weigh(t, 0)
                    weigh(t, 1)
                    if t + 1 < T:
                        values(t + 1)
                    weigh(t, 2)
                    weigh(t, 3)
                    turn_heads(t)
            project(T - 1)
            turn(0, 8)
            turn(1, 8)
            for part, (_, _, _, n, before) in enumerate(parts):
                if part == 1:
                    turn(0, 16)
                    turn(1, 16)
                    pe.wait_ge(S["r_lo"], 2)
                    for t in range(T):
                        pe.wait_ge(S["y_lo2"], 16 + 4 * (t // 4) + 4)
                        tok = slice((t % 4) * P, (t % 4) * P + P)
                        if t >= 2:
                            pe.wait_ge(S["lg_ok"], t - 1)
                        for k in range(KD):
                            ins = mm3(KV[t % 2][:, 0:32], pair(lambda s_: yT[t // 4][:, s_, k, tok]), pair(lambda s_: rws[:, s_, k]), k == 0, k == KD - 1)
                        ins.then_inc(S["lg_mm"], 1)
                        pe.wait_ge(S["di_ok"], t + 1)
                        if t >= 1:
                            pe.wait_ge(S["idx_ok"], t)
                        nc.tensor.matmul(SC[0][:, 0:P], onesr[:], didx, start=True, stop=True).then_inc(S["idx_mm"], 1)
                for h in range(2):
                    c0 = before + n * h

                    def up(c, par):
                        pe.wait_ge(S["w1_lo"], c + (c0 + 1))
                        if isinstance(c, int) and c == 0:
                            pe.wait_ge(S["y_lo2"], (8 if part == 0 else 16) + 8)
                        if not (isinstance(c, int) and c0 + c < 2):
                            pe.wait_ge(S["hact"], c + (c0 - 1))
                        for k in range(KD):
                            ins = mm3(pb[5 + par][:], pair(lambda s_: w1c[:, par, s_, k * P:(k + 1) * P]), pair(lambda s_: yT[h][:, s_, k]), k == 0, k == KD - 1)
                        ins.then_inc(S["hmm"], 1)

                    def down(c, par, first, last):
                        pe.wait_ge(S["hh_lo"], c + (c0 + 1))
                        pe.wait_ge(S["w2_lo"], c + (c0 + 1))
                        for t in range(4):
                            ins = mm3(pb[t][:], pair(lambda s_: hh[:, par, s_, t * P:(t + 1) * P]), pair(lambda s_: w2c[:, par, s_]), first, last)
                        ins.then_inc(S["f_mm"], 1)

                    if part == 0 and h == 1:
                        pe.wait_ge(S["x3_ok"], 4)
                    if part == 1:
                        pe.wait_ge(S["one_ok"], 1)
                        if h == 1:
                            pe.wait_ge(S["fin_out1"], 4)
                        for t in range(4):
                            tt = slice((4 * h + t) * P, (4 * h + t + 1) * P)
                            nc.tensor.matmul(pb[t][:], oneh[0:32, tt], e2s[0:32, 0], start=True, stop=False)
                            nc.tensor.matmul(pb[t][:], oneh[0:32, tt], e2s[0:32, 1], start=False, stop=False)
                    up(0, 0)

                    def step(c, par):
                        if isinstance(c, int) and c == n - 1:
                            down(c, par, False, True)
                            return
                        up(c + 1, 1 - par)
                        down(c, par, part == 0 and isinstance(c, int) and c == 0, False)
                    chunk_loop(pe, n, step)

        def interleaved(key_step, T_, W_, O_):
            key_step(0)
            T_(0)
            T_(1)
            T_(2)
            W_(0)
            T_(3)
            W_(1)
            O_(0)
            key_step(1)
            T_(4)
            W_(2)
            T_(5)
            W_(3)
            O_(1)
            key_step(2)
            T_(6)
            W_(4)
            T_(7)
            W_(5)
            O_(2)
            key_step(3)
            W_(6)
            W_(7)
            O_(3)

        def nothing(*_):
            pass

        @block.sync
        def _(sp):
            for t in range(0, T, 2):
                sp.dma_start(xs[:, t:t + 2, :], x.rearrange("(t p) d -> p t d", p=P)[:, t:t + 2, :]).then_inc(S[f"x_in{t // 2}"], 16)
            sp.dma_start(cs[:], consts).then_inc(S["cs_in"], 16)
            sp.dma_start(bo_bc, bo.partition_broadcast(P)).then_inc(S["bo_in"], 16)
            for n, (dst, src) in enumerate(((l1w, ln1w), (l1b, ln1b), (l2w, ln2w), (l2b, ln2b), (b1s, b1), (e1s, e1))):
                sp.dma_start(dst, src).then_inc(S["cols_in"], 16)
            sp.dma_start(rbs[:], rb.partition_broadcast(P)).then_inc(S["cols_in"], 16)
            sp.dma_start(wq_raw, Wq.rearrange("(k p) n -> p k n", p=P)).then_inc(S["wq_in"], 16)
            for dst, src in ((bq_s, bq), (bk_s, bk), (bv_s, bv)):
                sp.dma_start(dst[:], src).then_inc(S["bias_in"], 16)
            sp.dma_start(wk_raw, Wk.rearrange("(k p) n -> p k n", p=P)).then_inc(S["wk_in"], 16)
            sp.dma_start(wv_raw, Wv.rearrange("(k p) n -> p k n", p=P)).then_inc(S["wv_in"], 16)

            def load(b, par):
                if not (isinstance(b, int) and b < 2):
                    sp.wait_ge(S["y_lo"], b - 1)
                sp.dma_start(yraw[:, par], ctxT.rearrange("b (k p) n -> b p k n", p=P)[bass.ds(b, 1)]
                             .rearrange("b p k n -> (b p) k n") if not isinstance(b, int) else
                             ctxT.rearrange("b (k p) n -> b p k n", p=P)[b]).then_inc(S[f"y_in{par}"], 16)
            load(0, 0)
            load(1, 1)
            with sp.Fori(0, LOOPS) as i:
                load(2 * i + 2, 0)
                load(2 * i + 3, 1)
            sp_tail(sp)

        @block.gpsimd
        def _(pool):
            g = nc.gpsimd
            g.memset(pw[:], -0.5).then_inc(S["ms_ok"], 1)
            pool.wait_ge(S["ms_ok"], 1)
            pool.wait_ge(S["cs_in"], 16)
            pool.wait_ge(S["eps_ok"], 1)
            g.tensor_tensor(rstd[:], rstd[:], pw[:], ALU.pow).then_inc(S["rstd_ok"], 1)
            pool.wait_ge(S["wq_hi"], 1)
            g.tensor_tensor(wq[:, 1], wq_raw, wq[:, 0].bitcast(F32), ALU.subtract).then_inc(S["wq_lo"], 1)
            pool.wait_ge(S["wkv_hi"], 2)
            g.tensor_tensor(wv[:, 1], wv_raw, wv[:, 0].bitcast(F32), ALU.subtract).then_inc(S["wkv_lo"], 1)

            def split_y(b, par):
                pool.wait_ge(S[f"y_in{par}"], ((b - par) // 2 + 1) * 16 if isinstance(b, int) else b * 8 + (16 - 8 * par))
                if not (isinstance(b, int) and b < 2):
                    pool.wait_ge(S["kv_mm"], 8 * b - 8)
                pool.nop(nofuse=True)
                g.tensor_copy(y[:, par, 0], yraw[:, par]).then_inc(S["y_hi"], 1)
                pool.wait_ge(S["y_hi"], b + 1)
                g.tensor_tensor(y[:, par, 1], yraw[:, par], y[:, par, 0].bitcast(F32), ALU.subtract).then_inc(S["y_lo"], 1)

            def normalise(b):
                for hg in range(HG):
                    pool.wait_ge(S["rs_ok"], 4 * b + hg + 1)
                    pool.nop(nofuse=True)
                    for hp in (2 * hg, 2 * hg + 1):
                        g.tensor_scalar(probs[:, hp], probs[:, hp], rs[:, hp:hp + 1], 1.0, ALU.mult, ALU.mult).then_inc(S["norm_ok"], 1)
            def split_out(b, par):
                pool.wait_ge(S["pv_out"], 4 * b + 4)
                pool.wait_ge(S["pv_out2"], 4 * b + 4)
                pool.nop(nofuse=True)
                cols_ = bass.ds(b * SQ, SQ)
                g.tensor_copy(aT[:, 0, :, cols_], attnT[:, par]).then_inc(S["aT_hi"], 1)
                pool.wait_ge(S["aT_hi"], b + 1)
                pool.nop(nofuse=True)
                g.tensor_tensor(aT[:, 1, :, cols_], attnT[:, par], aT[:, 0, :, cols_].bitcast(F32), ALU.subtract).then_inc(S["aT_lo"], 1)
            split_y(0, 0)
            pool.wait_ge(S["bo_in"], 16)
            pool.wait_ge(S["xn_ok"], T)
            for t in range(T):
                g.tensor_tensor(xs[:, t], xs[:, t], bo_bc, ALU.add).then_inc(S["xb_ok"], 1)
            split_y(1, 1)
            normalise(0)
            with pool.Fori(0, LOOPS) as i:
                split_y(2 * i + 2, 0)
                split_out(2 * i, 0)
                normalise(2 * i + 1)
                split_y(2 * i + 3, 1)
                split_out(2 * i + 1, 1)
                normalise(2 * i + 2)
            split_out(NB - 2, 0)
            normalise(NB - 1)
            split_out(NB - 1, 1)
            pool_tail(pool)

        @block.scalar
        def _(act):
            a = nc.scalar
            act.wait_ge(S["wq_in"], 16)
            a.copy(wq[:, 0], wq_raw).then_inc(S["wq_hi"], 1)
            act.wait_ge(S["wk_in"], 16)
            a.copy(wk[:, 0], wk_raw).then_inc(S["wkv_hi"], 1)
            act.wait_ge(S["wv_in"], 16)
            a.copy(wv[:, 0], wv_raw).then_inc(S["wkv_hi"], 1)
            for t in range(T):
                act.wait_ge(S["xnT_mm"], t + 1)
                a.copy(xnT[:, 0, :, t * P:(t + 1) * P], TR[t % 2][:].rearrange("p (k n) -> p k n", k=KD)).then_inc(S["xnT_hi"], 1)

            def proj_hi(b, which, n):
                act.wait_ge(S["kv_mm"], 8 * b + 4 * which + n + 1)
                if which == 0:
                    if n == 0 and not (isinstance(b, int) and b == 0):
                        act.wait_ge(S["s_mm"], 8 * b)
                    a.activation(kT[:, 0, n], KV[n % 2][:], ACT.Identity, bias=bk_s[:, n:n + 1]).then_inc(S["kv_hi"], 1)
                else:
                    if n == 0 and not (isinstance(b, int) and b == 0):
                        act.wait_ge(S["pv_mm"], 4 * b)
                    a.copy(v[:, 0, n], KV[n % 2][:]).then_inc(S["kv_hi"], 1)

            def probs_hi(b, n):
                act.wait_ge(S["tr_mm"], 8 * b + n + 1)
                a.copy(pT[n % 4][:, 0], RING[n % 4][:]).then_inc(S["pT_hi"], 1)

            def out_evac(b, par, hg):
                if hg == 0 and not (isinstance(b, int) and b < 2):
                    act.wait_ge(S["aT_lo"], b - 1)
                act.wait_ge(S["pv_mm"], 4 * b + hg + 1)
                for j in range(2):
                    q = slice(32 * j, 32 * j + 32)
                    ins = a.activation(attnT[q, par, hg], PV[hg % 2][q, j * SQ:(j + 1) * SQ], ACT.Identity, bias=bv_s[q, hg:hg + 1])
                ins.then_inc(S["pv_out"], 1)

            def exps(b):
                for hp in range(8):
                    act.wait_ge(S["nmx_ok"], 8 * b + hp + 1)
                    if hp == 0 and not (isinstance(b, int) and b == 0):
                        act.wait_ge(S["tr_mm"], 8 * b)
                    a.activation(probs[:, hp], RING[hp % 4][:], ACT.Exp, bias=nmx[:, hp:hp + 1],
                                 accum_out=sums[:, hp:hp + 1]).then_inc(S["exp_ok"], 1)

            def body(b, par):
                first = isinstance(b, int) and b == 0
                act.wait_ge(S["bias_in"], 48) if first else None
                if first:
                    for n in range(4):
                        proj_hi(b, 0, n)
                else:
                    interleaved(lambda n: proj_hi(b, 0, n), lambda n: probs_hi(b - 1, n), nothing,
                                lambda hg: out_evac(b - 1, 1 - par, hg))
                for n in range(4):
                    proj_hi(b, 1, n)
                exps(b)
            over_batches(act, body)
            interleaved(nothing, lambda n: probs_hi(NB - 1, n), nothing, lambda hg: out_evac(NB - 1, 1, hg))
            act_tail(act)

        @block.vector
        def _(dve):
            d = nc.vector
            for t in range(T):
                dve.wait_ge(S[f"x_in{t // 2}"], 16)
                d.bn_stats(st[:, 6 * (t % 2):6 * (t % 2) + 6], xs[:, t]).then_inc(S["st_ok"], 1)
                dve.wait_ge(S["st_ok"], t + 1)
                d.bn_aggr(mv[:, 2 * t:2 * t + 2], st[:, 6 * (t % 2):6 * (t % 2) + 6]).then_inc(S["mv_ok"], 1)
            dve.wait_ge(S["mv_ok"], T)
            mvv = mv[:].rearrange("p (t c) -> p t c", c=2)
            d.tensor_scalar(rstd[:], mvv[:, :, 1], EPS, None, ALU.add).then_inc(S["eps_ok"], 1)
            dve.wait_ge(S["rstd_ok"], 1)

            def xnT_low(t):
                dve.wait_ge(S["xnT_hi"], t + 1)
                d.tensor_tensor(xnT[:, 1, :, t * P:(t + 1) * P], TR[t % 2][:].rearrange("p (k n) -> p k n", k=KD),
                                xnT[:, 0, :, t * P:(t + 1) * P].bitcast(F32), ALU.subtract).then_inc(S["xnT_lo"], 1)
            for t in range(T):
                if t >= 2:
                    dve.wait_ge(S["xnT_mm"], t - 1)
                d.tensor_scalar(xn[:, t % 2], xs[:, t], mv[:, 2 * t:2 * t + 1], rstd[:, t:t + 1],
                                ALU.subtract, ALU.mult).then_inc(S["xn_ok"], 1)
                if t >= 1:
                    xnT_low(t - 1)
            xnT_low(T - 1)
            dve.wait_ge(S["wkv_hi"], 2)
            d.tensor_tensor(wk[:, 1], wk_raw, wk[:, 0].bitcast(F32), ALU.subtract).then_inc(S["wk_lo"], 1)
            dve.wait_ge(S["wk_lo"], 1)
            dve.wait_ge(S["bias_in"], 48)
            dve.wait_ge(S["cs_in"], 16)
            dve.wait_ge(S["wkv_lo"], 1)
            for n in range(2 * HG):
                m, h = n % HG, n // HG
                dve.wait_ge(S["q_mm"], n + 1)
                d.tensor_scalar(qT[:, m, h * 512:(h + 1) * 512], KV[n % 2][:], bq_s[:, m:m + 1], SCALE,
                                ALU.add, ALU.mult).then_inc(S["q_ok"], 1)
            dve.wait_ge(S["q_ok"], 2 * HG)

            def proj_lo(b, which, n):
                dve.wait_ge(S["kv_hi"], 8 * b + 4 * which + n + 1)
                if which == 0:
                    d.scalar_tensor_tensor(out=kT[:, 1, n], in0=KV[n % 2][:], scalar=bk_s[:, n:n + 1],
                                           in1=kT[:, 0, n].bitcast(F32), op0=ALU.add, op1=ALU.subtract).then_inc(S["kv_lo"], 1)
                else:
                    d.tensor_tensor(v[:, 1, n], KV[n % 2][:], v[:, 0, n].bitcast(F32), ALU.subtract).then_inc(S["kv_lo"], 1)

            def spread_q(b, par):
                if not (isinstance(b, int) and b < 2):
                    dve.wait_ge(S["s_mm"], 8 * b - 8)
                src = qT[:, :, bass.ds(b * SQ, SQ)]
                for j in range(2):
                    d.tensor_scalar(qbd[:, par, 0, :, j * SQ:(j + 1) * SQ], src, half[:, j:j + 1], None, ALU.mult).then_inc(S["qbd_hi"], 1)
                for j in range(2):
                    dve.wait_ge(S["qbd_hi"], 2 * b + j + 1)
                    d.scalar_tensor_tensor(out=qbd[:, par, 1, :, j * SQ:(j + 1) * SQ], in0=src, scalar=half[:, j:j + 1],
                                           in1=qbd[:, par, 0, :, j * SQ:(j + 1) * SQ].bitcast(F32),
                                           op0=ALU.mult, op1=ALU.subtract).then_inc(S["qbd_ok"], 1)

            def probs_lo(b, n):
                dve.wait_ge(S["pT_hi"], 8 * b + n + 1)
                d.tensor_tensor(pT[n % 4][:, 1], RING[n % 4][:], pT[n % 4][:, 0].bitcast(F32), ALU.subtract).then_inc(S["pT_lo"], 1)

            def out_low_rows(b, par, hg):
                if hg == 0 and not (isinstance(b, int) and b < 2):
                    dve.wait_ge(S["aT_lo"], b - 1)
                dve.wait_ge(S["pv_mm"], 4 * b + hg + 1)
                for j in range(2, 4):
                    q = slice(32 * j, 32 * j + 32)
                    ins = d.tensor_scalar(attnT[q, par, hg], PV[hg % 2][q, j * SQ:(j + 1) * SQ], bv_s[q, hg:hg + 1], None, ALU.add)
                ins.then_inc(S["pv_out2"], 1)

            def maxima(b):
                for hp in range(8):
                    dve.wait_ge(S["s_mm"], 8 * b + hp + 1)
                    d.reduce_max(mx[:, hp:hp + 1], RING[hp % 4][:], AX).then_inc(S["mx_ok"], 1)
                    dve.wait_ge(S["mx_ok"], 8 * b + hp + 1)
                    d.tensor_scalar(nmx[:, hp:hp + 1], mx[:, hp:hp + 1], -1.0, None, ALU.mult).then_inc(S["nmx_ok"], 1)
                    if hp >= 2 and hp % 2 == 0:
                        reciprocals(b, hp // 2 - 1)
                reciprocals(b, 3)

            def reciprocals(b, hg):
                dve.wait_ge(S["exp_ok"], 8 * b + 2 * hg + 2)
                if not (isinstance(b, int) and b == 0) and hg == 0:
                    dve.wait_ge(S["norm_ok"], 8 * b)
                d.reciprocal(rs[:, 2 * hg:2 * hg + 2], sums[:, 2 * hg:2 * hg + 2]).then_inc(S["rs_ok"], 1)

            def body(b, par):
                if isinstance(b, int) and b == 0:
                    for n in range(4):
                        proj_lo(b, 0, n)
                else:
                    interleaved(lambda n: proj_lo(b, 0, n), lambda n: probs_lo(b - 1, n), nothing,
                                lambda hg: out_low_rows(b - 1, 1 - par, hg))
                spread_q(b, par)
                for n in range(4):
                    proj_lo(b, 1, n)
                maxima(b)
            over_batches(dve, body)
            interleaved(nothing, lambda n: probs_lo(NB - 1, n), nothing, lambda hg: out_low_rows(NB - 1, 1, hg))
            dve_tail(dve)

        @block.tensor
        def _(pe):
            def mm3(dst, w, m, first, last):
                nc.tensor.matmul(dst, w[1], m[0], start=first, stop=False)
                nc.tensor.matmul(dst, w[0], m[1], start=False, stop=False)
                return nc.tensor.matmul(dst, w[0], m[0], start=False, stop=last)

            pe.wait_ge(S["cs_in"], 16)
            for t in range(T):
                pe.wait_ge(S["xn_ok"], t + 1)
                if t >= 2:
                    pe.wait_ge(S["xnT_lo"], t - 1)
                for k in range(KD):
                    ins = nc.tensor.transpose(TR[t % 2][:, k * P:(k + 1) * P], xn[:, t % 2, k * P:(k + 1) * P], ident)
                ins.then_inc(S["xnT_mm"], 1)
            pe.wait_ge(S["wq_lo"], 1)
            for n in range(2 * HG):
                m, h = n % HG, n // HG
                pe.wait_ge(S["xnT_lo"], 4 * h + 4)
                if n >= 2:
                    pe.wait_ge(S["q_ok"], n - 1)
                for k in range(KD):
                    ins = mm3(KV[n % 2][:], [wq[:, s, k, m * P:(m + 1) * P] for s in range(2)],
                              [xnT[:, s, k, h * 512:(h + 1) * 512] for s in range(2)], k == 0, k == KD - 1)
                ins.then_inc(S["q_mm"], 1)
            pe.wait_ge(S["q_ok"], 2 * HG)
            pe.wait_ge(S["wkv_lo"], 1)
            pe.wait_ge(S["wk_lo"], 1)

            def proj(b, par, which, n):
                if not (isinstance(b, int) and b == 0 and which == 0 and n < 2):
                    pe.wait_ge(S["kv_lo"], 8 * b + 4 * which + n - 1)
                if which == 0 and n == 0:
                    pe.wait_ge(S["y_lo"], b + 1)
                for k in range(KC):
                    ys = [y[:, par, s, k] for s in range(2)]
                    if which == 0:
                        ins = mm3(KV[n % 2][:], [wk[:, s, k, n * P:(n + 1) * P] for s in range(2)], ys, k == 0, k == KC - 1)
                    else:
                        ins = mm3(KV[n % 2][:], [z[:, n * P:(n + 1) * P] for z in ys], [wv[:, s, k] for s in range(2)],
                                  k == 0, k == KC - 1)
                ins.then_inc(S["kv_mm"], 1)

            def scores(b, par):
                pe.wait_ge(S["qbd_ok"], 2 * b + 2)
                for hp in range(8):
                    if hp < 4 and hp == 0:
                        pe.wait_ge(S["kv_lo"], 8 * b + 4)
                    if hp >= 4:
                        pe.wait_ge(S["exp_ok"], 8 * b + hp - 3)
                    elif not (isinstance(b, int) and b == 0):
                        pe.wait_ge(S["pT_lo"], 8 * b)
                    r = slice(64 * (hp % 2), 64 * (hp % 2) + 64)
                    mm3(RING[hp % 4][:], [qbd[r, par, s, hp // 2] for s in range(2)],
                        [kT[r, s, hp // 2] for s in range(2)], True, True).then_inc(S["s_mm"], 1)

            def transposes(b, n):
                hg = n // 2
                if n % 2 == 0:
                    pe.wait_ge(S["norm_ok"], 8 * b + 2 * hg + 2)
                if n < 4:
                    pe.wait_ge(S["exp_ok"], 8 * b + 5 + n)
                else:
                    pe.wait_ge(S["pT_lo"], 8 * b + n - 3)
                for c in range(2):
                    for j in range(2):
                        kc = 2 * (n % 2) + c
                        ins = nc.tensor.transpose(RING[n % 4][:, c * 256 + j * P:c * 256 + (j + 1) * P],
                                                  probs[:, 2 * hg + j, kc * P:(kc + 1) * P], ident)
                ins.then_inc(S["tr_mm"], 1)

            def weigh(b, n):
                hg = n // 2
                pe.wait_ge(S["pT_lo"], 8 * b + n + 1)
                if n % 2 == 0 and not (isinstance(b, int) and b == 0 and hg < 2):
                    pe.wait_ge(S["pv_out"], 4 * b + hg - 1)
                    pe.wait_ge(S["pv_out2"], 4 * b + hg - 1)
                for c in range(2):
                    kc = 2 * (n % 2) + c
                    ins = mm3(PV[hg % 2][:, 0:256], [v[:, s, kc, hg * P:(hg + 1) * P] for s in range(2)],
                              [pT[n % 4][:, s, c * 256:(c + 1) * 256] for s in range(2)], kc == 0, kc == 3)
                if n % 2 == 1:
                    ins.then_inc(S["pv_mm"], 1)

            def body(b, par):
                if isinstance(b, int) and b == 0:
                    for n in range(4):
                        proj(b, par, 0, n)
                else:
                    interleaved(lambda n: proj(b, par, 0, n), lambda n: transposes(b - 1, n), lambda n: weigh(b - 1, n), nothing)
                for n in range(4):
                    proj(b, par, 1, n)
                scores(b, par)
            over_batches(pe, body)
            interleaved(nothing, lambda n: transposes(NB - 1, n), lambda n: weigh(NB - 1, n), nothing)
            pe_tail(pe, mm3)


def layout(inputs):
    a = {n: np.asarray(v) for n, v in inputs.items()}
    P = 128
    X, T_ = "L0_xattn_", "L0_attn_"
    F_ = "L0_ffn_"
    c = np.ascontiguousarray
    cols = lambda v: c(v.reshape(-1, P).T)

    def spread(w, kinds):
        t = np.zeros((512, 4, 8, 4), np.float32)
        for r in range(kinds):
            t[:, :, r] = w[:, :, 0].T.reshape(512, 4, 4)
        return c(t.reshape(512, P))
    p = np.arange(P)
    consts = np.zeros((P, 2 * P + 44), np.float32)
    consts[:, 0:P] = np.eye(P)
    consts[:, P:2 * P] = (p[:, None] // 64 == p[None] // 64) & (p[:, None] <= p[None])
    consts[:, 2 * P:2 * P + 32] = np.arange(32)
    for j in range(2):
        consts[:, 2 * P + 32 + j] = (p // 32) % 2 == j
    for j in range(4):
        consts[:, 2 * P + 34 + j] = (p % 32 < 8) & (p % 4 == j)
    consts[:, 2 * P + 38] = np.pi / 2
    used, low = p % 32 < 8, p % 8 < 4
    consts[:, 2 * P + 40] = np.where(used & ~low, -np.pi / 4, 0)
    consts[:, 2 * P + 41] = used & low
    consts[:, 2 * P + 42] = np.where(used & low, np.pi / 4, 0)
    consts[:, 2 * P + 43] = used & ~low
    consts[:, 2 * P + 39] = p
    return {
        "x": c(a["x"].reshape(-1, 512)), "ctxT": c(a["ctx_768"].transpose(0, 2, 1)),
        "Wq": a[X + "Wq"], "bq": cols(a[X + "bq"]), "Wk": a[X + "Wk"], "bk": cols(a[X + "bk"]),
        "Wv": a[X + "Wv"], "bv": cols(a[X + "bv"]), "Wo": a[X + "Wo"], "bo": a[X + "bo"],
        "WQ": spread(a[T_ + "W_Q"], 2), "WK": spread(a[T_ + "W_K"], 2),
        "WV": c(a[T_ + "W_V"].transpose(1, 0, 2).reshape(512, 1024)),
        "WO": c(a[T_ + "W_O"].transpose(2, 1, 0).reshape(1024, 512)),
        "ln1w": cols(a[T_ + "ln1_w"]), "ln1b": cols(a[T_ + "ln1_b"]), "ln2w": cols(a[T_ + "ln2_w"]), "ln2b": cols(a[T_ + "ln2_b"]),
        "W1": a[T_ + "W1"], "b1": cols(a[T_ + "b1"]), "W2": a[T_ + "W2"], "b2": a[T_ + "b2"],
        "rw": c(a[F_ + "router_w"].T), "rb": a[F_ + "router_b"],
        "E1": a[F_ + "weights1"], "e1": c(a[F_ + "bias1"].T), "E2": a[F_ + "weights2"], "e2": a[F_ + "bias2"],
        "consts": consts,
    }


def kernel(**inputs):
    import concourse.bacc as bacc
    from concourse import mybir as _mybir
    from concourse.bass_utils import run_bass_kernel_spmd

    arrays = layout(inputs)
    nc = bacc.Bacc("TRN2", target_bir_lowering=False, num_devices=1)
    args = [nc.dram_tensor(n, a.shape, _mybir.dt.from_np(a.dtype), kind="ExternalInput").ap() for n, a in arrays.items()]
    args.append(nc.dram_tensor("out", (1024, 512), F32, kind="ExternalOutput").ap())
    build(nc, *args)
    r = run_bass_kernel_spmd(nc, [arrays], core_ids=[0])
    return r.results[0]["out"].reshape(16, 64, 512)
```
